# Optimizing a Trainium2 kernel written in Bass

```python
import numpy as np
import jax
import jax.numpy as jnp

def _softmax(x, axis=-1):
    return jax.nn.softmax(x, axis=axis)

def _gelu(x):
    return jax.nn.gelu(x, approximate=True)

def _silu(x):
    return jax.nn.silu(x)

def _sigmoid(x):
    return jax.nn.sigmoid(x)

def _layernorm(x, axis=-1, eps=1e-05):
    m = jnp.mean(x, axis=axis, keepdims=True)
    v = jnp.var(x, axis=axis, keepdims=True)
    return (x - m) / jnp.sqrt(v + eps)

def _scatter_add(tgt, idx, src, axis=0):
    return tgt.at[idx].add(src)

def _segment_sum(src, seg, n):
    return jax.ops.segment_sum(src, seg, n)
kernel_name = 'mk_xattn_seq_d2_seqx_r8_70f1e6'

def setup_inputs(seed: int=0):
    np.random.seed(seed)
    _w = jnp.asarray

    def _rec_inputs():
        import jax
        import jax.numpy as jnp
        _rk = jax.random.key(seed)
        x = -0.0005146 + 1 * jax.random.normal(jax.random.fold_in(_rk, 1), (32, 64, 256), jnp.float32)
        _lenS = 64 - jax.random.randint(jax.random.fold_in(_rk, 7), (32,), 0, max(1, 64 // 4) + 1, jnp.int32)
        _lenS2 = 64 - jax.random.randint(jax.random.fold_in(_rk, 8), (32,), 0, max(1, 64 // 4) + 1, jnp.int32)
        _ctx_2048P = jax.random.normal(jax.random.fold_in(_rk, 11), (32, 16, 256), jnp.float32)
        _ctx_2048c = jax.random.dirichlet(jax.random.fold_in(_rk, 511), 0.3 * jnp.ones((16,), jnp.float32), (32, 64))
        _ctx_2048t = jnp.einsum('bsk,bkd->bsd', _ctx_2048c, _ctx_2048P)
        _ctx_2048t = _ctx_2048t * jax.lax.rsqrt(jnp.mean(jnp.square(_ctx_2048t)) + 1e-12) * 0.953939
        ctx_2048 = -0.000392918 + 0.999932 * (_ctx_2048t + 0.3 * jax.random.normal(jax.random.fold_in(_rk, 611), (32, 64, 256), jnp.float32))
        _validS = jnp.arange(64)[None, :] < _lenS[:, None]
        _validS2 = jnp.arange(64)[None, :] < _lenS2[:, None]
        _causal = jnp.tril(jnp.ones((64, 64), dtype=bool))
        mask_BxS2_ik0 = jnp.where(jnp.broadcast_to(_validS2[:, :], (32, 64)), 0, 1).astype(jnp.int32)
        return (x, ctx_2048, mask_BxS2_ik0)
    x, ctx_2048, mask_BxS2_ik0 = _rec_inputs()

    def _L0_xattn_setup():
        import jax, jax.numpy as jnp
        import numpy as np
        B, P, K, H, NH = (4, 256, 32, 256, 16)
        DH = H // NH
        EPS = 1e-06

        def rmsnorm(x, w):
            var = jnp.mean(jnp.square(x), axis=-1, keepdims=True)
            return x * jax.lax.rsqrt(var + EPS) * w
        key = jax.random.key(seed)
        ks = jax.random.split(key, 12)
        s = 0.02
        return {'x': jax.random.normal(ks[0], (B, P, H), jnp.float32), 'latents': jax.random.normal(ks[1], (B, K, H), jnp.float32), 'attention_mask': jax.random.randint(ks[2], (B, P), 0, 2, jnp.int32), 'q_w': s * jax.random.normal(ks[3], (H, H), jnp.float32), 'q_b': jnp.zeros((H,), jnp.float32), 'kv_w': s * jax.random.normal(ks[4], (H, 2 * H), jnp.float32), 'kv_b': jnp.zeros((2 * H,), jnp.float32), 'out_w': s * jax.random.normal(ks[5], (H, H), jnp.float32), 'out_b': jnp.zeros((H,), jnp.float32), 'postnorm_w': jnp.ones((H,), jnp.float32), 'mlp_w1': s * jax.random.normal(ks[6], (H, 4 * H), jnp.float32), 'mlp_b1': jnp.zeros((4 * H,), jnp.float32), 'mlp_w2': s * jax.random.normal(ks[7], (4 * H, H), jnp.float32), 'mlp_b2': jnp.zeros((H,), jnp.float32)}
    _L0_xattn_all = _L0_xattn_setup()
    _L0_xattn_in = {k: v for k, v in _L0_xattn_all.items() if k in ('q_w', 'q_b', 'kv_w', 'kv_b', 'out_w', 'out_b', 'postnorm_w', 'mlp_w1', 'mlp_b1', 'mlp_w2', 'mlp_b2')}
    del _L0_xattn_all

    def _L1_xattn_setup():
        import jax, jax.numpy as jnp
        import numpy as np
        N, C, S, S2, H, CTX = (4, 64, 256, 256, 8, 64)
        EPS = 1e-05
        key = jax.random.key(seed)
        ks = jax.random.split(key, 6)
        sd = lambda fan: 1.0 / np.sqrt(fan)
        return {'input': jax.random.normal(ks[0], (N, C, S), jnp.float32), 'context': jax.random.normal(ks[1], (N, CTX, S2), jnp.float32), 'gamma': jnp.ones((C,), jnp.float32), 'beta': jnp.zeros((C,), jnp.float32), 'Wq': jax.random.normal(ks[2], (C * H, C), jnp.float32) * sd(C), 'bq': jnp.zeros((C * H,), jnp.float32), 'Wkv': jax.random.normal(ks[3], (C * H * 2, CTX), jnp.float32) * sd(CTX), 'bkv': jnp.zeros((C * H * 2,), jnp.float32), 'Wo': jax.random.normal(ks[4], (C, C * H), jnp.float32) * sd(C * H), 'bo': jnp.zeros((C,), jnp.float32)}
    _L1_xattn_all = _L1_xattn_setup()
    _L1_xattn_in = {k: v for k, v in _L1_xattn_all.items() if k in ('gamma', 'beta', 'Wq', 'bq', 'Wkv', 'bkv', 'Wo', 'bo')}
    del _L1_xattn_all
    return {'x': x, 'ctx_2048': ctx_2048, 'mask_BxS2_ik0': mask_BxS2_ik0, 'L0_xattn_q_w': _L0_xattn_in['q_w'], 'L0_xattn_q_b': _L0_xattn_in['q_b'], 'L0_xattn_kv_w': _L0_xattn_in['kv_w'], 'L0_xattn_kv_b': _L0_xattn_in['kv_b'], 'L0_xattn_out_w': _L0_xattn_in['out_w'], 'L0_xattn_out_b': _L0_xattn_in['out_b'], 'L0_xattn_postnorm_w': _L0_xattn_in['postnorm_w'], 'L0_xattn_mlp_w1': _L0_xattn_in['mlp_w1'], 'L0_xattn_mlp_b1': _L0_xattn_in['mlp_b1'], 'L0_xattn_mlp_w2': _L0_xattn_in['mlp_w2'], 'L0_xattn_mlp_b2': _L0_xattn_in['mlp_b2'], 'L1_xattn_gamma': _L1_xattn_in['gamma'], 'L1_xattn_beta': _L1_xattn_in['beta'], 'L1_xattn_Wq': _L1_xattn_in['Wq'], 'L1_xattn_bq': _L1_xattn_in['bq'], 'L1_xattn_Wkv': _L1_xattn_in['Wkv'], 'L1_xattn_bkv': _L1_xattn_in['bkv'], 'L1_xattn_Wo': _L1_xattn_in['Wo'], 'L1_xattn_bo': _L1_xattn_in['bo']}

def reference(x, ctx_2048, mask_BxS2_ik0, L0_xattn_q_w, L0_xattn_q_b, L0_xattn_kv_w, L0_xattn_kv_b, L0_xattn_out_w, L0_xattn_out_b, L0_xattn_postnorm_w, L0_xattn_mlp_w1, L0_xattn_mlp_b1, L0_xattn_mlp_w2, L0_xattn_mlp_b2, L1_xattn_gamma, L1_xattn_beta, L1_xattn_Wq, L1_xattn_bq, L1_xattn_Wkv, L1_xattn_bkv, L1_xattn_Wo, L1_xattn_bo):
    import jax
    import jax.numpy as jnp

    def _L0_xattn_ref(x, latents, attention_mask, q_w, q_b, kv_w, kv_b, out_w, out_b, postnorm_w, mlp_w1, mlp_b1, mlp_w2, mlp_b2):
        import jax, jax.numpy as jnp
        import numpy as np
        B, P, K, H, NH = (4, 256, 32, 256, 16)
        DH = H // NH
        EPS = 1e-06

        def rmsnorm(x, w):
            var = jnp.mean(jnp.square(x), axis=-1, keepdims=True)
            return x * jax.lax.rsqrt(var + EPS) * w
        b, p, _ = x.shape
        k_len = latents.shape[1]
        residual = latents
        h = jnp.concatenate([x, latents], axis=1)
        q = (latents @ q_w + q_b).reshape(b, k_len, NH, DH)
        kv = (h @ kv_w + kv_b).reshape(b, p + k_len, NH, DH, 2)
        kmat, v = (kv[..., 0], kv[..., 1])
        attn = jnp.einsum('bkhd,bnhd->bhkn', q, kmat) / DH
        full_mask = jnp.concatenate([attention_mask.astype(bool), jnp.ones((b, k_len), bool)], axis=-1)
        attn = jnp.where(full_mask[:, None, None, :], attn, -jnp.inf)
        attn = jax.nn.softmax(attn.astype(jnp.float32), axis=-1).astype(q.dtype)
        attn_out = jnp.einsum('bhkn,bnhd->bkhd', attn, v).reshape(b, k_len, H)
        attn_out = attn_out @ out_w + out_b + residual
        out = rmsnorm(attn_out, postnorm_w)
        out = jax.nn.gelu(out @ mlp_w1 + mlp_b1) @ mlp_w2 + mlp_b2
        return out + residual

    def _L1_xattn_ref(input, context, gamma, beta, Wq, bq, Wkv, bkv, Wo, bo):
        import jax, jax.numpy as jnp
        import numpy as np
        N, C, S, S2, H, CTX = (4, 64, 256, 256, 8, 64)
        EPS = 1e-05
        n, c, s = input.shape
        h = H
        mu = jnp.mean(input, axis=(1, 2), keepdims=True)
        var = jnp.var(input, axis=(1, 2), keepdims=True)
        xn = (input - mu) * jax.lax.rsqrt(var + EPS)
        xn = xn * gamma[None, :, None] + beta[None, :, None]
        q = jnp.einsum('oc,ncs->nos', Wq, xn) + bq[None, :, None]
        kv = jnp.einsum('od,nds->nos', Wkv, context) + bkv[None, :, None]
        q = q.reshape(n, h, c, s).transpose(0, 1, 3, 2)
        kv = kv.reshape(n, 2 * h, c, -1).transpose(0, 1, 3, 2)
        k, v = (kv[:, :h], kv[:, h:])
        scale = c ** (-0.25)
        att = jax.nn.softmax(jnp.einsum('nhqc,nhkc->nhqk', q * scale, k * scale), axis=-1)
        y = jnp.einsum('nhqk,nhkc->nhqc', att, v)
        y = y.transpose(0, 1, 3, 2).reshape(n, h * c, s)
        out = jnp.einsum('co,nos->ncs', Wo, y) + bo[None, :, None]
        return input + out
    x = _L0_xattn_ref(ctx_2048, x, mask_BxS2_ik0, L0_xattn_q_w, L0_xattn_q_b, L0_xattn_kv_w, L0_xattn_kv_b, L0_xattn_out_w, L0_xattn_out_b, L0_xattn_postnorm_w, L0_xattn_mlp_w1, L0_xattn_mlp_b1, L0_xattn_mlp_w2, L0_xattn_mlp_b2)
    x = _L1_xattn_ref(x, ctx_2048, L1_xattn_gamma, L1_xattn_beta, L1_xattn_Wq, L1_xattn_bq, L1_xattn_Wkv, L1_xattn_bkv, L1_xattn_Wo, L1_xattn_bo)
    return x

_drawn_inputs = setup_inputs


def setup_inputs(seed=0):
    import zlib

    import numpy as np

    out = dict(_drawn_inputs(seed))
    spreads = {'L0_xattn_q_b': (0.0, 0.8),
     'L0_xattn_kv_b': (0.0, 0.8),
     'L0_xattn_out_b': (0.0, 0.664),
     'L0_xattn_postnorm_w': (1.0, 0.6),
     'L0_xattn_mlp_b1': (0.0, 0.1),
     'L0_xattn_mlp_b2': (0.0, 0.1),
     'L1_xattn_gamma': (1.0, 0.2),
     'L1_xattn_beta': (0.0, 0.1),
     'L1_xattn_bq': (0.0, 0.1),
     'L1_xattn_bkv': (0.0, 0.1),
     'L1_xattn_bo': (0.0, 0.1)}
    factors = {'L0_xattn_q_w': 8.0, 'L0_xattn_kv_w': 8.0, 'L0_xattn_out_w': 8.0}
    for name, (base, spread) in spreads.items():
        noise = np.random.default_rng([zlib.crc32(name.encode()), seed]).standard_normal(out[name].shape)
        drawn = base * np.exp(spread * noise) if base else spread * noise
        out[name] = jnp.asarray(drawn.astype(out[name].dtype))
    for name, factor in factors.items():
        out[name] = (out[name] * factor).astype(out[name].dtype)
    return out
```

```python
from contextlib import ExitStack

import concourse.bass as bass
from concourse import mybir

F32 = mybir.dt.float32
F32R = mybir.dt.float32r
BF16 = mybir.dt.bfloat16
I32 = mybir.dt.int32
ALU = mybir.AluOpType
ACT = mybir.ActivationFunctionType
AX = mybir.AxisListType

NB = 32
GB = 4
NG = NB // GB
NH0 = 16
NH1 = 8
NEG = -1.0e30

SM = dict(qb=(0, 2), kb=(2, 2), vb=(4, 2), b1=(6, 8), pw=(14, 2), gamma=(16, 1), beta=(17, 1),
          bo=(18, 1), bq=(19, 8), bk=(27, 8), bv=(35, 8), par=(43, 2), hm=(45, 8), ob=(53, 256), b2=(309, 256),
          ident=(565, 128), avg=(693, 128), mh=(821, 2))
SMW = 823


class Engine:

    def __init__(self, sem):
        self.sem = sem
        self.n = 0
        self.todo = []
        self.seen = {}

    def do(self, emit, *after, inc=True):
        waits = []
        for t in after:
            if t is None:
                continue
            sem, v = t
            if self.seen.get(id(sem), 0) < v:
                self.seen[id(sem)] = v
                waits.append((sem, v))
        if inc:
            self.n += 1
        self.todo.append((waits, emit, self.sem if inc else None, 1))
        return (self.sem, self.n)

    def dma(self, emit, sem, count, *after):
        self.do(emit, *after, inc=False)
        waits, emit, _, _ = self.todo[-1]
        self.todo[-1] = (waits, emit, sem, 16)
        return (sem, 16 * count)

    def play(self, eng):
        for waits, emit, sem, k in self.todo:
            for s, v in waits:
                eng.wait_ge(s, v)
            if emit is None:
                continue
            ins = emit(eng)
            if sem is not None:
                ins.then_inc(sem, k)


def build(nc, hT, xn_d, ctx_d, msk_d, qw_d, kvw_d, ow_d, w1_d, w2_d, l1_d, sm_d, out_d):
    with ExitStack() as es:
        def sb(name, shape, dt=F32):
            return es.enter_context(nc.sbuf_tensor(name, shape, dt))

        def sem(name):
            return es.enter_context(nc.semaphore(name))

        bank = [es.enter_context(nc.psum_tensor(f"bank{i}", [128, 512], F32)) for i in range(8)]

        PE, VE, SC, PO, SY = (Engine(sem(n)) for n in ("s_pe", "s_ve", "s_sc", "s_po", "s_sy"))

        small = sb("small", [128, SMW])

        def sm(name):
            a, n = SM[name]
            return small[:, a:a + n]

        wq = [sb(f"wq{i}", [128, 2, 256], F32R) for i in range(2)]
        wk = [sb(f"wk{i}", [128, 2, 256], F32R) for i in range(2)]
        wv = [sb(f"wv{i}", [128, 2, 256], F32R) for i in range(2)]
        wo = [sb(f"wo{i}", [128, 2, 256], F32R) for i in range(2)]
        w1 = [sb(f"w1{i}", [128, 2, 1024], F32R) for i in range(2)]
        w2 = [sb(f"w2{i}", [128, 8, 256], F32R) for i in range(2)]
        MM = [sb(f"MM{i}", [128, 512], F32R) for i in range(2)]
        WS = sb("WS", [128, 512], F32R)
        uu = sb("uu", [128, 8])
        cbias = sb("cbias", [128, 1])
        obt = sb("obt", [128, 256])
        mski = sb("mski", [1, GB, 64], I32)
        mrow = [sb(f"mrow{i}", [128, GB, 128], BF16) for i in range(2)]
        onesb = sb("onesb", [128, 128], BF16)

        hraw = sb("hraw", [128, 2, GB, 128])
        hh = [sb(f"hh{i}", [128, 2, GB, 128], F32R) for i in range(2)]
        xnat = sb("xnat", [128, 2, 256])
        xo = sb("xo", [128, 2, 256])
        kT = sb("kT", [128, 2, GB, 128])
        qT = sb("qT", [128, 2, GB, 64])
        vv = sb("vv", [128, GB, 256])
        QDb = sb("QDb", [128, 2, 2, 8, 64])
        QD = [QDb[:, i] for i in range(2)]
        E0 = [sb(f"E0{i}", [128, 8, 128]) for i in range(2)]
        PT0 = sb("PT0", [128, 8, 128])
        nm0 = [sb(f"nm0{i}", [128, 8]) for i in range(2)]
        sum0 = [sb(f"sum0{i}", [128, 8]) for i in range(2)]
        rs0 = [sb(f"rs0{i}", [128, 8]) for i in range(2)]
        tmpo = [sb(f"tmpo{i}", [128, 2, 64]) for i in range(2)]
        AO = sb("AO", [128, 2, GB, 64])
        aos = [sb(f"aos{i}", [128, 2, GB, 64], F32R) for i in range(2)]
        yy = sb("yy", [128, 2, 256])
        ysq = sb("ysq", [128, 256])
        ss = sb("ss", [128, 2])
        rr = sb("rr", [128, 2])
        ynT = [sb(f"ynT{i}", [128, 2, 256], F32R) for i in range(2)]
        hm = sb("hm", [128, 8, 256])
        gs = [sb(f"gs{i}", [128, 4, 256], F32R) for i in range(2)]
        X1 = [sb(f"X1{i}", [128, 256]) for i in range(4)]

        craw = sb("craw", [128, GB, 256])
        CH = [sb(f"CH{i}", [128, GB, 256], F32R) for i in range(2)]
        CL = [sb(f"CL{i}", [128, GB, 256], F32R) for i in range(2)]
        st6 = sb("st6", [128, 6])
        mv = sb("mv", [128, 2])
        mu = sb("mu", [128, 1])
        dd = sb("dd", [128, 1])
        ee = sb("ee", [128, 1])
        rstd = sb("rstd", [128, 1])
        aa = sb("aa", [128, 1])
        mb = sb("mb", [128, 1])
        bb = sb("bb", [128, 1])
        xnb = sb("xnb", [128, 2, 256])
        xnrm = [xnb[:, i] for i in range(2)]
        XS = [sb(f"XS{i}", [128, 256], F32R) for i in range(2)]
        QS = [sb(f"QS{i}", [128, 8, 256], F32R) for i in range(2)]
        VW = [sb(f"VW{i}", [128, 2, 512]) for i in range(2)]
        E1b = sb("E1b", [128, 4, 2, 256])
        E1 = [E1b[:, i] for i in range(4)]
        nm1 = [sb(f"nm1{i}", [128, 2]) for i in range(4)]
        sum1 = [sb(f"sum1{i}", [128, 2]) for i in range(4)]
        rs1 = [sb(f"rs1{i}", [128, 2]) for i in range(4)]
        PT1b = sb("PT1b", [128, 3, 2, 256])
        PT1 = [PT1b[:, i] for i in range(3)]

        sto = xnb[:, :, :]
        stk, stq = PT1b[:, 0:2], PT1b[:, 2]
        stw1 = hm[:, :, :].rearrange("p k n -> p (k n)").rearrange("p (k n) -> p k n", k=2)
        stage = QDb[:, :, :, :, :].rearrange("p a b c d -> p (a b c d)").rearrange("p (k n) -> p k n", k=8)
        l1w = E1b[0:64, :, :, :].rearrange("p w a n -> p w (a n)")
        y1 = [sb(f"y1{i}", [128, 256]) for i in range(2)]

        class Ring:
            def __init__(self, banks):
                self.banks = banks
                self.free = [() for _ in banks]
                self.i = 0

            def take(self):
                for _ in self.banks:
                    k = self.i % len(self.banks)
                    self.i += 1
                    if self.free[k] is not None:
                        break
                fr, self.free[k] = self.free[k], None
                return k, self.banks[k], fr

        RS, RT, RG = Ring([bank[0], bank[1]]), Ring([bank[2], bank[3]]), Ring([bank[5], bank[6], bank[7]])
        OB = bank[4]

        def mm(out, lhsT, rhs, start, stop, *after, inc=False):
            return PE.do(lambda e: e.matmul(out, lhsT, rhs, start=start, stop=stop, skip_group_check=True), *after,
                         inc=inc)

        def three(out, a, b, start, stop, *after, inc=False):
            mm(out, a[0], b[0], start, False, *after)
            mm(out, a[0], b[1], False, False)
            return mm(out, a[1], b[0], False, stop, inc=inc)

        def f(ap):
            return ap.bitcast(F32)

        d_sm, d_q, d_kv, d_o, d_w1, d_w2, d_l1, d_mk = (sem(n) for n in
                                                        ("d_sm", "d_q", "d_kv", "d_o", "d_w1", "d_w2", "d_l1", "d_mk"))
        d_h, d_x, d_c, d_out = sem("d_h"), sem("d_x"), sem("d_c"), [sem("d_out0"), sem("d_out1")]
        t_small = SY.dma(lambda e: e.dma_start(small[:, :], sm_d), d_sm, 1)

        free_hraw, free_x, free_craw = (), (), ()
        loads = {}

        def load_group(g, after_h=(), after_x=(), after_c=()):
            th = SY.dma(lambda e: e.dma_start(hraw[:, :, :, :], hT[g].rearrange("p (k b t) -> p k b t", k=2, b=GB)),
                        d_h, g + 1, *after_h)
            tx = SY.dma(lambda e: e.dma_start(xnat[:, :, :], xn_d[g].rearrange("(u p) s -> p u s", p=128)),
                        d_x, g + 1, *after_x)
            src = ctx_d[g * GB:(g + 1) * GB].rearrange("b c s -> c b s")
            SY.dma(lambda e: e.dma_start(craw[0:64, :, :], src), d_c, 2 * g + 1, *after_c)
            tc = SY.dma(lambda e: e.dma_start(craw[64:128, :, :], src), d_c, 2 * g + 2)
            tk_ = SY.dma(lambda e: e.dma_start(mski[:, :, :], msk_d[:, g * GB:(g + 1) * GB, :]), d_mk, g + 1)
            loads[g] = (th, tx, tc, tk_)

        load_group(0)
        SY.dma(lambda e: e.dma_start(stk[:, 0, :, :], kvw_d[0].rearrange("(k p) n -> p k n", p=128)), d_kv, 1)
        t_kvw = SY.dma(lambda e: e.dma_start(stk[:, 1, :, :], kvw_d[1].rearrange("(k p) n -> p k n", p=128)), d_kv, 2)
        t_qw = SY.dma(lambda e: e.dma_start(stq[:, :, :], qw_d.rearrange("(k p) n -> p k n", p=128)), d_q, 1)
        t_ow = SY.dma(lambda e: e.dma_start(sto[:, :, :], ow_d.rearrange("(k p) n -> p k n", p=128)), d_o, 1)
        t_w1 = SY.dma(lambda e: e.dma_start(stw1[:, :, :], w1_d.rearrange("(k p) n -> p k n", p=128)), d_w1, 1)
        t_w2 = SY.dma(lambda e: e.dma_start(stage[:, :, :], w2_d.rearrange("(k p) n -> p k n", p=128)), d_w2, 1)
        t_l1 = SY.dma(lambda e: e.dma_start(l1w[:, :, :], l1_d.rearrange("w o n -> o w n")), d_l1, 1)

        def split(hi, lo, src, *after):
            t = VE.do(lambda e: e.tensor_copy(hi, src), *after)
            return VE.do(lambda e: e.tensor_tensor(lo, src, f(hi), ALU.subtract), t)

        t_ones = PO.do(lambda e: e.memset(onesb[:, :], 1.0))
        PO.do(lambda e: e.memset(mrow[0][:, :, :], 0.0))
        t_mz = PO.do(lambda e: e.memset(mrow[1][:, :, :], 0.0))
        t_hh0 = split(hh[0][:, :, :, :], hh[1][:, :, :, :], hraw[:, :, :, :], loads[0][0])
        t_wk = split(wk[0][:, :, :], wk[1][:, :, :], stk[:, 0, :, :], t_kvw)
        t_wv = split(wv[0][:, :, :], wv[1][:, :, :], stk[:, 1, :, :], t_kvw)
        t_wq = split(wq[0][:, :, :], wq[1][:, :, :], stq[:, :, :], t_qw)
        ready = {}

        def weights_late():
            ready["wo"] = split(wo[0][:, :, :], wo[1][:, :, :], sto[:, :, :], t_ow)
            k, b, fr = RG.take()
            vb = sm("vb")
            mm(b[:, 0:256], vb[:, 0:1].to_broadcast([128, 128]), sto[:, 0, :], True, False, t_ow, t_small, *fr)
            t = mm(b[:, 0:256], vb[:, 1:2].to_broadcast([128, 128]), sto[:, 1, :], False, True, inc=True)
            ready["obt"] = VE.do(lambda e: e.tensor_tensor(obt[:, :], b[:, 0:256], sm("ob"), ALU.add), t)
            RG.free[k] = (ready["obt"],)
            yield
            pw = sm("pw")
            ts = [VE.do(lambda e, k=k: e.tensor_scalar(stw1[:, k, :], stw1[:, k, :], pw[:, k:k + 1], None, ALU.mult),
                        t_w1, t_small) for k in range(2)]
            ready["w1"] = split(w1[0][:, :, :], w1[1][:, :, :], stw1[:, :, :], *ts)
            ready["w2"] = split(w2[0][:, :, :], w2[1][:, :, :], stage[:, :, :], t_w2)
            yield
            W = l1w[:, :, :].rearrange("o w (h c) -> o w h c", h=8)

            def both(b, col, n, lhsT, rhs, start, stop, *after, inc=False):
                for a in range(0, 128, 64):
                    t = mm(b[a:a + 64, col:col + n], lhsT, rhs, start, stop, *after, inc=inc and a == 64)
                return t
            k1, bM, f1 = RG.take()
            for h in range(8):
                tM = both(bM, h * 64, 64, W[:, 0, h, :], W[:, 1, h, :], h == 0, h == 7,
                        t_l1, *f1, inc=h == 7)
            k2, bV, f2 = RG.take()
            for h in range(8):
                tV = both(bV, h * 64, 64, W[:, 2, h, :], W[:, 3, h, :], h == 0, h == 7, *f2, inc=h == 7)
            k3, bU, f3 = RG.take()
            bq, bv = sm("bq"), sm("bv")
            for h in range(8):
                both(bU, h, 1, W[:, 1, h, :], bq[0:64, h:h + 1], h == 0, h == 7, t_small, *f3)
            for h in range(8):
                tU = both(bU, 8, 1, W[:, 3, h, :], bv[0:64, h:h + 1], False, h == 7, inc=h == 7)
            t = VE.do(lambda e: e.tensor_scalar(MM[0][:, :], bM[:, :], 0.125, None, ALU.mult), tM)
            ready["M"] = VE.do(lambda e: e.scalar_tensor_tensor(MM[1][:, :], bM[:, :], 0.125, f(MM[0][:, :]),
                                                                ALU.mult, ALU.subtract), t)
            RG.free[k1] = (ready["M"],)
            t1 = VE.do(lambda e: e.tensor_copy(WS[:, :], bV[:, :]), tV)
            ready["V"] = VE.do(lambda e: e.tensor_tensor(WS[64:128, :], bV[64:128, :], f(WS[64:128, :]),
                                                         ALU.subtract), t1)
            RG.free[k2] = (ready["V"],)
            VE.do(lambda e: e.tensor_scalar(uu[:, :], bU[:, 0:8], 0.125, None, ALU.mult), tU)
            ready["u"] = VE.do(lambda e: e.tensor_tensor(cbias[:, :], bU[:, 8:9], sm("bo"), ALU.add))
            RG.free[k3] = (ready["u"],)
            yield

        st = dict(hh=t_hh0, hh_free=(), kT_free=(), qT_free=(), vv_free=(), ao_free=(), aos_free=(), xo_free=(),
                  yn_free=(), ynT_free=(), gs_free=(), hm_free=(), gl_free=())
        qd_free, e0_free, pt0_free = [None, None], [None, None], [None, None]
        x1_ready, x1_free = {}, [(), (), (), ()]
        c_ready, c_free = {}, [(), ()]

        def layer0(g):
            th, tx, tc, tkm = loads[g]
            t_mrow = VE.do(lambda e: e.tensor_scalar(mrow[g % 2][0:1, :, 0:64], mski[:, :, :], 0.0, NEG, ALU.is_equal,
                                                     ALU.mult), tkm, t_mz, qd_free[(GB - 1) % 2])
            if g == 0:
                thh = st["hh"]
            else:
                thh = split(hh[0][:, :, :, :], hh[1][:, :, :, :], hraw[:, :, :, :], th, *st["hh_free"])
            t_xo = None
            tk = []
            for m in range(2):
                k, b, fr = RG.take()
                for kt in range(2):
                    a = [w[:, kt, m * 128:(m + 1) * 128] for w in wk]
                    t = three(b[:, :], a, [x[:, kt, :, :] for x in hh], kt == 0, kt == 1, thh, t_wk, *fr, inc=kt == 1)
                kb = sm("kb")
                tk.append(SC.do(lambda e, m=m, b=b: e.activation(kT[:, m, :, :], b[:, :].rearrange(
                    "p (b t) -> p b t", b=GB), ACT.Identity, bias=kb[:, m:m + 1], scale=1.0), t, t_small,
                    *st["kT_free"]))
                RG.free[k] = (tk[-1],)
                yield
            k, b, fr = RG.take()
            for m in range(2):
                for kt in range(2):
                    a = [w[:, kt, m * 128:(m + 1) * 128] for w in wq]
                    t = three(b[:, m * 256:(m + 1) * 256], a, [x[:, kt, :, 64:128] for x in hh],
                              m == 0 and kt == 0, kt == 1, t_wq, *fr, inc=kt == 1)
            for m in range(2):
                qb = sm("qb")
                tq = VE.do(lambda e, m=m, b=b: e.tensor_scalar(
                    qT[:, m, :, :], b[:, m * 256:(m + 1) * 256].rearrange("p (b t) -> p b t", b=GB),
                    qb[:, m:m + 1], 0.0625, ALU.add, ALU.mult), t, t_small, *st["qT_free"])
            RG.free[k] = (tq,)
            yield
            tv = []
            for u in range(2):
                k, b, fr = RG.take()
                for i in range(2):
                    for kt in range(2):
                        a = [x[:, kt, 2 * u + i, :] for x in hh]
                        t = three(b[:, i * 256:(i + 1) * 256], a, [w[:, kt, :] for w in wv],
                                  i == 0 and kt == 0, kt == 1, t_wv, *fr, inc=i == 1 and kt == 1)
                tv.append(SC.do(lambda e, u=u, b=b: e.copy(
                    vv[:, 2 * u:2 * u + 2, :], b[:, :].rearrange("p (b n) -> p b n", b=2)), t, *st["vv_free"]))
                RG.free[k] = (tv[-1],)
                yield
            st["hh_free"] = (t,)
            if g == 0:
                yield from weights_late()
            t_xo = PO.do(lambda e: e.tensor_tensor(xo[:, :, :], xnat[:, :, :], obt[:, :].unsqueeze(1).to_broadcast(
                [128, 2, 256]), ALU.add), tx, ready["obt"], *st["xo_free"])
            t_xb = PO.do(lambda e: e.tensor_tensor(xnat[:, :, :], xnat[:, :, :], sm("b2").unsqueeze(1).to_broadcast(
                [128, 2, 256]), ALU.add), t_xo)
            yield
            tAO, keep = [], {}

            def at_q(b):
                r = b % 2
                for m in range(2):
                    t = PO.do(lambda e, m=m: e.tensor_tensor(
                        QD[r][:, m, :, :], qT[:, m, b, :].unsqueeze(1).to_broadcast([128, 8, 64]),
                        sm("hm").unsqueeze(2).to_broadcast([128, 8, 64]), ALU.mult), tq, qd_free[r], ready["w2"])
                keep["qd", b] = t

            def at_s(b, m):
                r = b % 2
                if True:
                    k, pb, fr = RG.take()
                    mm(pb[:, :], onesb[:, :], mrow[g % 2][:, b, :].unsqueeze(1).to_broadcast([128, 4, 128]), True, False,
                       t_mrow, t_ones, keep["qd", b], tk[m], *fr)
                    for j in range(4):
                        t = mm(pb[:, j * 128:(j + 1) * 128], QD[r][:, m, 2 * j:2 * j + 2, :], kT[:, m, b, :],
                               False, j == 3, inc=j == 3)
                    if m == 1:
                        qd_free[r] = t
                    t = VE.do(lambda e, m=m, pb=pb: e.tensor_reduce(
                        nm0[r][:, 4 * m:4 * m + 4], pb[:, :].rearrange("p (j t) -> p j t", j=4), AX.X, ALU.max,
                        negate=True), t, e0_free[r])
                    for j in range(4):
                        jj = 4 * m + j
                        t2 = SC.do(lambda e, j=j, jj=jj, pb=pb: e.activation(
                            E0[r][:, jj, :], pb[:, j * 128:(j + 1) * 128], ACT.Exp, bias=nm0[r][:, jj:jj + 1],
                            scale=1.0, accum_out=sum0[r][:, jj:jj + 1]), t, e0_free[r])
                    RG.free[k] = (t2,)
                    keep["e", b, m] = t2

            def at_n(b):
                r = b % 2
                t = VE.do(lambda e: e.reciprocal(rs0[r][:, :], sum0[r][:, :]), keep["e", b, 1])
                keep["n", b] = PO.do(lambda e: e.tensor_tensor(
                    E0[r][:, :, :], E0[r][:, :, :], rs0[r][:, :].unsqueeze(2).to_broadcast([128, 8, 128]),
                    ALU.mult), t)

            def at_t(b, m):
                r = b % 2
                k, pb, fr = RG.take()
                for j in range(4):
                    t = PE.do(lambda e, j=j: e.transpose(pb[:, j * 128:(j + 1) * 128], E0[r][:, 4 * m + j, :],
                                                         sm("ident")), keep["n", b], *fr, inc=j == 3)
                if m == 1:
                    e0_free[r] = t
                tt = SC.do(lambda e: e.copy(PT0[:, 4 * m:4 * m + 4, :], pb[:, :].rearrange(
                    "p (j t) -> p j t", j=4)), t, pt0_free[0])
                RG.free[k] = (tt,)
                keep["t", b, m] = tt

            def at_v(b):
                r = b % 2
                k, pb, fr = RG.take()
                for m in range(2):
                    for j in range(4):
                        t = mm(pb[32 * j:32 * j + 32, m * 128:(m + 1) * 128],
                               vv[:, b, 128 * m + 32 * j:128 * m + 32 * j + 32], PT0[:, 4 * m + j, :],
                               m == 0, m == 1, tv[b // 2], keep["t", b, 1], *fr, inc=m == 1 and j == 3)
                pt0_free[0] = t
                o = pb[:, 0:256].rearrange("p (m h q) -> p m h q", m=2, h=2)
                par = sm("par")
                t2 = SC.do(lambda e: e.activation(tmpo[r][:, :, :], o[:, :, 0, :], ACT.Copy, bias=0.0,
                                                  scale=par[:, 0:1]), t, keep.get(("ao", b - 2)))
                t3 = VE.do(lambda e: e.scalar_tensor_tensor(AO[:, :, b, :], o[:, :, 1, :], par[:, 1:2],
                                                            tmpo[r][:, :, :], ALU.mult, ALU.add), t2, *st["ao_free"])
                RG.free[k] = (t3,)
                keep["ao", b] = t3

            for i in range(GB + 3):
                if i < GB:
                    at_q(i)
                if 0 <= i - 2 < GB:
                    at_n(i - 2)
                yield
                for m in range(2):
                    if 0 <= i - 1 < GB:
                        at_s(i - 1, m)
                        yield
                if 0 <= i - 2 < GB:
                    for m in range(2):
                        at_t(i - 2, m)
                    yield
                    at_v(i - 2)
                    yield
            st["qT_free"] = (keep["qd", GB - 1],)
            st["kT_free"] = (qd_free[(GB - 1) % 2],)
            st["vv_free"] = (pt0_free[0],)
            t = split(aos[0][:, :, :, :], aos[1][:, :, :, :], AO[:, :, :, :], keep["ao", GB - 1], *st["aos_free"])
            st["ao_free"] = (t,)
            yield
            k, pb, fr = RG.take()
            for u in range(2):
                for kt in range(2):
                    a = [x[:, kt, 2 * u:2 * u + 2, :] for x in aos]
                    t1 = three(pb[:, u * 256:(u + 1) * 256], a, [w[:, kt, :] for w in wo], u == 0 and kt == 0,
                               kt == 1, t, ready["wo"], *fr, inc=u == 1 and kt == 1)
            st["aos_free"] = (t1,)
            t = VE.do(lambda e, pb=pb: e.tensor_tensor(yy[:, :, :], pb[:, :].rearrange("p (u n) -> p u n", u=2), xo[:, :, :],
                                                ALU.add), t1, t_xo)
            RG.free[k] = (t,)
            st["xo_free"] = (t,)
            for u in range(2):
                tt = VE.do(lambda e, u=u: e.tensor_tensor_reduce(
                    ysq[:, :], yy[:, u, :], yy[:, u, :], 1.0 / 256, 0.0, ALU.mult, ALU.add, ss[:, u:u + 1]), t)
                t = tt
            t = VE.do(lambda e: e.tensor_scalar(rr[:, :], ss[:, :], 1e-6, None, ALU.add), t)
            t = PO.do(lambda e: e.tensor_tensor(rr[:, :], rr[:, :], sm("mh"), ALU.pow), t)
            yield
            for u in range(2):
                tn = VE.do(lambda e, u=u: e.tensor_scalar(yy[:, u, :], yy[:, u, :], rr[:, u:u + 1], None, ALU.mult),
                           t, *st["yn_free"])
            yield
            k, pb, fr = RG.take()
            for kt in range(2):
                for u in range(2):
                    t = PE.do(lambda e, kt=kt, u=u, pb=pb: e.transpose(pb[:, kt * 256 + u * 128:kt * 256 + u * 128 + 128],
                                                                yy[:, u, kt * 128:(kt + 1) * 128], sm("ident")),
                              tn, *fr, inc=kt == 1 and u == 1)
            st["yn_free"] = (t,)
            src = pb[:, :].rearrange("p (k t) -> p k t", k=2)
            t1 = SC.do(lambda e: e.copy(ynT[0][:, :, :], src), t, *st["ynT_free"])
            tT = VE.do(lambda e: e.tensor_tensor(ynT[1][:, :, :], src, f(ynT[0][:, :, :]), ALU.subtract), t1)
            RG.free[k] = (tT,)
            yield
            b1 = sm("b1")
            for c in range(4):
                k, pb, fr = RG.take()
                for i in range(2):
                    m = 2 * c + i
                    for kt in range(2):
                        a = [w[:, kt, m * 128:(m + 1) * 128] for w in w1]
                        t = three(pb[:, i * 256:(i + 1) * 256], a, [x[:, kt, :] for x in ynT], i == 0 and kt == 0,
                                  kt == 1, tT, ready["w1"], *fr, inc=i == 1 and kt == 1)
                th_ = VE.do(lambda e, c=c, pb=pb: e.tensor_tensor(
                    hm[:, 2 * c:2 * c + 2, :], pb[:, :].rearrange("p (i t) -> p i t", i=2),
                    b1[:, 2 * c:2 * c + 2].unsqueeze(2).to_broadcast([128, 2, 256]), ALU.add), t, *st["hm_free"])
                RG.free[k] = (th_,)
                yield
            st["ynT_free"] = (t,)
            tg = SC.do(lambda e: e.activation(hm[:, :, :], hm[:, :, :], ACT.Gelu_apprx_tanh), th_, *st["gl_free"])
            yield
            k, pb, fr = RG.take()
            for c in range(2):
                t = VE.do(lambda e, c=c: e.tensor_copy(gs[0][:, :, :], hm[:, 4 * c:4 * c + 4, :]), tg, *st["gs_free"])
                tgs = PO.do(lambda e, c=c: e.tensor_tensor(gs[1][:, :, :], hm[:, 4 * c:4 * c + 4, :],
                                                           f(gs[0][:, :, :]), ALU.subtract), t)
                yield
                for u in range(2):
                    for kt in range(4 * c, 4 * c + 4):
                        a = [x[:, kt % 4, u * 128:(u + 1) * 128] for x in gs]
                        t = three(pb[:, u * 256:(u + 1) * 256], a, [w[:, kt, :] for w in w2],
                                  kt == 0 and u == 0, kt == 7, tgs, ready["w2"], *fr, inc=kt % 4 == 3)
                st["gs_free"] = (t,)
                yield
            st["hm_free"] = (tgs,)
            for u in range(2):
                p = 2 * g + u
                x1_ready[p] = VE.do(lambda e, u=u, p=p: e.tensor_tensor(
                    X1[p % 4][:, :], pb[:, u * 256:(u + 1) * 256], xnat[:, u, :], ALU.add), t, t_xb, *x1_free[p % 4])
            RG.free[k] = (x1_ready[2 * g + 1],)
            cs = g % 2
            t1 = VE.do(lambda e: e.tensor_copy(CH[cs][:, :, :], craw[:, :, :]), tc, *c_free[cs])
            c_ready[g] = PO.do(lambda e: e.tensor_tensor(CL[cs][:, :, :], craw[:, :, :], f(CH[cs][:, :, :]),
                                                         ALU.subtract), t1, *c_free[cs])
            yield
            if g + 1 < NG:
                load_group(g + 1, (thh,), (x1_ready[2 * g + 1],), (c_ready[g], t_mrow))
            yield

        xn_ready, qs_ready, vw_ready = {}, {}, {}
        xnrm_free, xs_free, qs_free, vw_free = [(), ()], [(), ()], [(), ()], [(), ()]

        def norm_pair(p):
            x = X1[p % 4]
            t = VE.do(lambda e: e.bn_stats(st6[:, :], x[:, :]), x1_ready[p])
            tm = VE.do(lambda e: e.bn_aggr(mv[:, :], st6[:, :]), t)
            k, pb, fr = RG.take()
            t = mm(pb[:, 0:1], sm("avg"), mv[:, 0:1], True, True, tm, t_small, *fr, inc=True)
            yield
            tmu = VE.do(lambda e: e.tensor_copy(mu[:, :], pb[:, 0:1]), t)
            t = VE.do(lambda e: e.tensor_tensor(dd[:, :], mv[:, 0:1], mu[:, :], ALU.subtract), tmu)
            t = VE.do(lambda e: e.scalar_tensor_tensor(ee[:, :], dd[:, :], dd[:, 0:1], mv[:, 1:2], ALU.mult, ALU.add),
                      t)
            t = mm(pb[:, 2:3], sm("avg"), ee[:, :], True, True, t, inc=True)
            yield
            t = VE.do(lambda e: e.tensor_scalar(rstd[:, :], pb[:, 2:3], 1e-5, None, ALU.add), t)
            RG.free[k] = (t,)
            t = PO.do(lambda e: e.tensor_tensor(rstd[:, :], rstd[:, :], sm("mh")[:, 0:1], ALU.pow), t)
            yield
            t = VE.do(lambda e: e.tensor_tensor(aa[:, :], rstd[:, :], sm("gamma"), ALU.mult), t)
            t = VE.do(lambda e: e.tensor_tensor(mb[:, :], mu[:, :], aa[:, :], ALU.mult), t)
            t = VE.do(lambda e: e.tensor_tensor(bb[:, :], sm("beta"), mb[:, :], ALU.subtract), t)
            xn_ready[p] = VE.do(lambda e: e.tensor_scalar(xnrm[p % 2][:, :], x[:, :], aa[:, 0:1], bb[:, 0:1],
                                                          ALU.mult, ALU.add), t, *xnrm_free[p % 2])
            yield

        def prep(n):
            p, o, s, g, bg = n // 2, 64 * (n % 2), n % 2, n // GB, n % GB
            if n % 2 == 0:
                yield from norm_pair(p)
            q = 64 - o
            xr = xnrm[p % 2]
            t = SC.do(lambda e: e.copy(XS[s][o:o + 64, :], xr[o:o + 64, :]), xn_ready[p], *xs_free[s])
            txs = VE.do(lambda e: e.tensor_tensor(XS[s][q:q + 64, :], xr[o:o + 64, :], f(XS[s][o:o + 64, :]),
                                                  ALU.subtract), t)
            if n % 2 == 1:
                xnrm_free[p % 2] = (txs,)
            yield
            ch, cl = CH[g % 2], CL[g % 2]
            tv = []
            for j in range(2):
                k, pb, fr = RG.take()
                mm(pb[:, :], ch[:, bg, j * 128:(j + 1) * 128], WS[:, :], True, False, ready["V"], c_ready[g], *fr)
                t = mm(pb[:, :], cl[:, bg, j * 128:(j + 1) * 128], WS[:, :], False, True, inc=True)
                E = (SC, VE)[j]
                tv.append(E.do((lambda e, pb=pb: e.copy(VW[s][:, 0, :], pb[:, :])) if j == 0 else
                               (lambda e, pb=pb: e.tensor_copy(VW[s][:, 1, :], pb[:, :])), t, *vw_free[s]))
                RG.free[k] = (tv[-1],)
            vw_ready[n] = tv
            yield
            for c in range(2):
                k, pb, fr = RG.take()
                for i in range(2):
                    pr = 2 * c + i
                    sl = pb[:, i * 256:(i + 1) * 256]
                    mm(sl, MM[0][:, pr * 128:(pr + 1) * 128], XS[s][:, :], i == 0, False, txs, ready["M"],
                       ready["u"], *fr)
                    t = mm(sl, MM[1][:, pr * 128:(pr + 1) * 128], XS[s][:, :], False, True, inc=i == 1)
                where = [(4 * c + j, 64 * (j % 2), pb[64 * (j % 2):64 * (j % 2) + 64, 256 * (j // 2):256 * (j // 2) + 256])
                         for j in range(4)]
                for h, a, sl in where:
                    th = SC.do(lambda e, h=h, a=a, sl=sl: e.activation(
                        QS[s][a:a + 64, h, :], sl, ACT.Identity, bias=uu[a:a + 64, h:h + 1], scale=1.0),
                        t, *qs_free[s])
                for h, a, sl in where:
                    z = 64 - a
                    tl = VE.do(lambda e, h=h, a=a, z=z, sl=sl: e.scalar_tensor_tensor(
                        QS[s][z:z + 64, h, :], sl, uu[a:a + 64, h:h + 1], f(QS[s][a:a + 64, h, :]), ALU.add,
                        ALU.subtract), th, *qs_free[s])
                    qs_ready[n, h] = tl
                RG.free[k] = (tl,)
                yield
            xs_free[s] = (t,)

        e1_free, pt1_free, hs = [None] * 4, [None] * 3, {}
        o_free, y1_free, yo_free = [None, None], [None, None], [None, None]

        def stage_s(t_):
            n, h = divmod(t_, 8)
            s, g, bg, r = n % 2, n // GB, n % GB, t_ % 4
            k, pb, fr = RS.take()
            for i in range(2):
                a = QS[s][:, h, i * 128:(i + 1) * 128]
                mm(pb[:, i * 256:(i + 1) * 256], a, CH[g % 2][:, bg, :], i == 0, False, qs_ready[n, h], *fr)
                t = mm(pb[:, i * 256:(i + 1) * 256], a, CL[g % 2][:, bg, :], False, True, inc=i == 1)
            if h == 7:
                qs_free[s] = (t,)
                if bg == GB - 1:
                    hs["c", g] = t
            t = VE.do(lambda e: e.tensor_reduce(nm1[r][:, :], pb[:, :].rearrange("p (i t) -> p i t", i=2), AX.X,
                                                ALU.max, negate=True), t, e1_free[r])
            for i in range(2):
                t2 = SC.do(lambda e, i=i: e.activation(E1[r][:, i, :], pb[:, i * 256:(i + 1) * 256], ACT.Exp,
                                                       bias=nm1[r][:, i:i + 1], scale=1.0,
                                                       accum_out=sum1[r][:, i:i + 1]), t, e1_free[r])
            RS.free[k] = (t2,)
            hs["e", t_] = t2

        def stage_n(t_):
            r = t_ % 4
            t = VE.do(lambda e: e.reciprocal(rs1[r][:, :], sum1[r][:, :]), hs["e", t_])
            hs["n", t_] = PO.do(lambda e: e.tensor_tensor(
                E1[r][:, :, :], E1[r][:, :, :], rs1[r][:, :].unsqueeze(2).to_broadcast([128, 2, 256]), ALU.mult), t)

        def stage_t(t_):
            r, r3 = t_ % 4, t_ % 3
            k, pb, fr = RT.take()
            for j in range(2):
                for i in range(2):
                    t = PE.do(lambda e, i=i, j=j: e.transpose(
                        pb[:, j * 256 + i * 128:j * 256 + i * 128 + 128], E1[r][:, i, j * 128:(j + 1) * 128],
                        sm("ident")), hs["n", t_], *fr, inc=i == 1 and j == 1)
            e1_free[r] = t
            src = pb[:, :].rearrange("p (j t) -> p j t", j=2)
            if t_ % 4 == 3:
                t2 = SC.do(lambda e: e.copy(PT1[r3][:, :, :], src), t, pt1_free[r3])
            else:
                t2 = VE.do(lambda e: e.tensor_copy(PT1[r3][:, :, :], src), t, pt1_free[r3])
            RT.free[k] = (t2,)
            hs["t", t_] = t2

        def stage_v(t_):
            n, h = divmod(t_, 8)
            r3, s, c = t_ % 3, n % 2, 64 * (h % 2)
            o = OB[c:c + 64, s * 256:(s + 1) * 256]
            for j in range(2):
                t = mm(o, VW[s][:, j, h * 64:(h + 1) * 64], PT1[r3][:, j, :], h < 2 and j == 0, h >= 6 and j == 1,
                       hs["t", t_], vw_ready[n][j], o_free[0], inc=j == 1)
            pt1_free[r3] = t
            if h == 7:
                vw_free[s] = (t,)
                hs["v", n] = t

        def finish(n):
            p, a, s = n // 2, 64 * (n % 2), n % 2
            x = X1[p % 4]
            o = OB[:, s * 256:(s + 1) * 256]
            t = VE.do(lambda e: e.scalar_tensor_tensor(y1[p % 2][a:a + 64, :], o[a:a + 64, :], cbias[a:a + 64, 0:1],
                                                       x[a:a + 64, :], ALU.add, ALU.add), hs["v", n], yo_free[p % 2],
                      ready["u"])
            z = 64 - a
            t = VE.do(lambda e: e.tensor_tensor(y1[p % 2][a:a + 64, :], o[z:z + 64, :], y1[p % 2][a:a + 64, :],
                                                ALU.add), t, None)
            o_free[0] = t
            if s == 1:
                x1_free[p % 4] = (t,)
                yo_free[p % 2] = SY.dma(lambda e: e.dma_start(out_d[2 * p:2 * p + 2].rearrange("b c s -> (b c) s"),
                                                              y1[p % 2][:, :]), d_out[p % 2], p // 2 + 1, t)

        for _ in layer0(0):
            pass
        for _ in prep(0):
            pass
        bg0, bg1 = None, None
        T = NB * 8
        n0 = 0
        for t_ in range(T + 3):
            n, h = divmod(t_, 8)
            if t_ < T:
                if h == 0 and n % GB == 0 and n // GB + 1 < NG:
                    if n // GB >= 1:
                        c_free[(n // GB + 1) % 2] = (hs["c", n // GB - 1],)
                    bg0 = layer0(n // GB + 1)
                stage_s(t_)
            if 0 <= t_ - 1 < T:
                stage_n(t_ - 1)
            if bg0 is not None:
                for _ in range(2):
                    next(bg0, None)
                if h == 7 and n % GB == GB - 2:
                    for _ in bg0:
                        pass
                    bg0 = None
            if 0 <= t_ - 2 < T:
                stage_t(t_ - 2)
            if 0 <= t_ - 3 < T:
                stage_v(t_ - 3)
                if (t_ - 3) % 8 == 7:
                    finish((t_ - 3) // 8)
            if t_ < T and n + 1 < NB:
                if h == 0:
                    bg1 = prep(n + 1)
                if h >= 1:
                    next(bg1, None)
                if h == 7:
                    for _ in bg1:
                        pass

        SY.do(None, (d_out[0], 16 * (NB // 4)), (d_out[1], 16 * (NB // 4)), inc=False)

        block = es.enter_context(nc.Block())

        @block.sync
        def _(e):
            SY.play(e)

        @block.tensor
        def _(e):
            PE.play(e)

        @block.vector
        def _(e):
            VE.play(e)

        @block.scalar
        def _(e):
            SC.play(e)

        @block.gpsimd
        def _(e):
            PO.play(e)


def kernel(x, ctx_2048, mask_BxS2_ik0, L0_xattn_q_w, L0_xattn_q_b, L0_xattn_kv_w, L0_xattn_kv_b, L0_xattn_out_w,
           L0_xattn_out_b, L0_xattn_postnorm_w, L0_xattn_mlp_w1, L0_xattn_mlp_b1, L0_xattn_mlp_w2, L0_xattn_mlp_b2,
           L1_xattn_gamma, L1_xattn_beta, L1_xattn_Wq, L1_xattn_bq, L1_xattn_Wkv, L1_xattn_bkv, L1_xattn_Wo,
           L1_xattn_bo):
    import numpy as np
    import concourse.bacc as bacc
    from concourse.bass_utils import run_bass_kernel_spmd

    asc = np.ascontiguousarray
    x = np.asarray(x)
    ctx = np.asarray(ctx_2048)
    h = np.concatenate([ctx, x], axis=1).reshape(NG, GB, 128, 2, 128)
    hT = asc(h.transpose(0, 4, 3, 1, 2)).reshape(NG, 128, 2 * GB * 128)
    kvw = asc(np.asarray(L0_xattn_kv_w).reshape(256, 256, 2).transpose(2, 0, 1))
    kvb = np.asarray(L0_xattn_kv_b).reshape(256, 2)
    wkv = np.asarray(L1_xattn_Wkv).reshape(2, 8, 64, 64)

    def heads(w):
        return np.asarray(w).reshape(8, 64, 64).transpose(1, 0, 2).reshape(64, 512)
    l1 = asc(np.stack([heads(L1_xattn_Wq), heads(wkv[0]), heads(wkv[1]), heads(np.asarray(L1_xattn_Wo).T)]))

    small = np.zeros((128, SMW), np.float32)

    def put(name, a):
        o, n = SM[name]
        small[:, o:o + n] = a
    put("qb", np.asarray(L0_xattn_q_b).reshape(2, 128).T)
    put("kb", kvb[:, 0].reshape(2, 128).T)
    put("vb", kvb[:, 1].reshape(2, 128).T)
    put("b1", np.asarray(L0_xattn_mlp_b1).reshape(8, 128).T)
    put("pw", np.asarray(L0_xattn_postnorm_w).reshape(2, 128).T)

    def twice(a):
        a = np.asarray(a)
        return np.concatenate([a, a], axis=0)
    put("gamma", twice(L1_xattn_gamma)[:, None])
    put("beta", twice(L1_xattn_beta)[:, None])
    put("bo", twice(L1_xattn_bo)[:, None])
    put("bq", twice(np.asarray(L1_xattn_bq).reshape(8, 64).T))
    bkv = np.asarray(L1_xattn_bkv).reshape(2, 8, 64)
    put("bk", twice(bkv[0].T))
    put("bv", twice(bkv[1].T))
    p = np.arange(128)
    put("par", ((p[:, None] // 16) % 2 == np.arange(2)[None, :]).astype(np.float32))
    put("hm", (p[:, None] // 16 == np.arange(8)[None, :]).astype(np.float32))
    put("ob", np.asarray(L0_xattn_out_b)[None, :])
    put("b2", np.asarray(L0_xattn_mlp_b2)[None, :])
    put("mh", np.float32(-0.5))
    put("ident", np.eye(128, dtype=np.float32))
    put("avg", np.where(p[:, None] // 64 == p[None, :] // 64, np.float32(1 / 64), np.float32(0)))

    arrays = {
        "hT": hT, "xn": asc(x.reshape(NG, 256, 256)), "ctx": asc(ctx),
        "msk": asc(np.asarray(mask_BxS2_ik0)).reshape(1, NB, 64), "qw": asc(L0_xattn_q_w), "kvw": kvw,
        "ow": asc(L0_xattn_out_w), "w1": asc(L0_xattn_mlp_w1), "w2": asc(L0_xattn_mlp_w2), "l1": l1, "sm": small,
    }
    nc = bacc.Bacc("TRN2", target_bir_lowering=False, num_devices=1)
    args = [nc.dram_tensor(f"in_{k}", a.shape, mybir.dt.from_np(a.dtype), kind="ExternalInput").ap()
            for k, a in arrays.items()]
    out = nc.dram_tensor("out_0", (NB, 64, 256), F32, kind="ExternalOutput").ap()
    build(nc, *args, out)
    r = run_bass_kernel_spmd(nc, [{f"in_{k}": a for k, a in arrays.items()}], core_ids=[0])
    return r.results[0]["out_0"]
```

```python
from contextlib import ExitStack

import concourse.bass as bass
from concourse import mybir

F32 = mybir.dt.float32
F32R = mybir.dt.float32r
BF16 = mybir.dt.bfloat16
I32 = mybir.dt.int32
ALU = mybir.AluOpType
ACT = mybir.ActivationFunctionType
AX = mybir.AxisListType

NB = 32
GB = 4
NG = NB // GB
NH0 = 16
NH1 = 8
NEG = -1.0e30
CFG = (105, 26, 2, 3, 4, 5, 6)
PH = 1

SM = dict(qb=(0, 2), kb=(2, 2), vb=(4, 2), b1=(6, 8), pw=(14, 2), gamma=(16, 1), beta=(17, 1),
          bo=(18, 1), bq=(19, 8), bk=(27, 8), bv=(35, 8), par=(43, 2), hm=(45, 8), ob=(53, 256), b2=(309, 256),
          ident=(565, 128), avg=(693, 128), mh=(821, 2))
SMW = 823


class Engine:

    def __init__(self, sem):
        self.sem = sem
        self.n = 0
        self.todo = []
        self.seen = {}

    def do(self, emit, *after, inc=True):
        waits = []
        for t in after:
            if t is None:
                continue
            sem, v = t
            if self.seen.get(id(sem), 0) < v:
                self.seen[id(sem)] = v
                waits.append((sem, v))
        if inc:
            self.n += 1
        self.todo.append((waits, emit, self.sem if inc else None, 1))
        return (self.sem, self.n)

    def dma(self, emit, sem, count, *after):
        self.do(emit, *after, inc=False)
        waits, emit, _, _ = self.todo[-1]
        self.todo[-1] = (waits, emit, sem, 16)
        return (sem, 16 * count)

    def play(self, eng):
        for waits, emit, sem, k in self.todo:
            for s, v in waits:
                eng.wait_ge(s, v)
            if emit is None:
                continue
            ins = emit(eng)
            if sem is not None:
                ins.then_inc(sem, k)


def build(nc, hT, xn_d, ctx_d, msk_d, qw_d, kvw_d, ow_d, w1_d, w2_d, l1_d, sm_d, out_d):
    with ExitStack() as es:
        def sb(name, shape, dt=F32):
            return es.enter_context(nc.sbuf_tensor(name, shape, dt))

        def sem(name):
            return es.enter_context(nc.semaphore(name))

        bank = [es.enter_context(nc.psum_tensor(f"bank{i}", [128, 512], F32)) for i in range(8)]

        PE, VE, SC, PO, SY = (Engine(sem(n)) for n in ("s_pe", "s_ve", "s_sc", "s_po", "s_sy"))

        small = sb("small", [128, SMW])

        def sm(name):
            a, n = SM[name]
            return small[:, a:a + n]

        wq = [sb(f"wq{i}", [128, 2, 256], F32R) for i in range(2)]
        wk = [sb(f"wk{i}", [128, 2, 256], F32R) for i in range(2)]
        wv = [sb(f"wv{i}", [128, 2, 256], F32R) for i in range(2)]
        wo = [sb(f"wo{i}", [128, 2, 256], F32R) for i in range(2)]
        w1 = [sb(f"w1{i}", [128, 2, 1024], F32R) for i in range(2)]
        w2 = [sb(f"w2{i}", [128, 8, 256], F32R) for i in range(2)]
        MM = [sb(f"MM{i}", [128, 512], F32R) for i in range(2)]
        WS = sb("WS", [128, 512], F32R)
        uu = sb("uu", [128, 8])
        cbias = sb("cbias", [128, 1])
        obt = sb("obt", [128, 256])
        mski = sb("mski", [1, GB, 64], I32)
        mrow = [sb(f"mrow{i}", [128, GB, 128], BF16) for i in range(2)]
        onesb = sb("onesb", [128, 128], BF16)

        hraw = sb("hraw", [128, 2, GB, 128])
        hh = [sb(f"hh{i}", [128, 2, GB, 128], F32R) for i in range(2)]
        xnat = sb("xnat", [128, 2, 256])
        xo = sb("xo", [128, 2, 256])
        kT = sb("kT", [128, 2, GB, 128])
        qT = sb("qT", [128, 2, GB, 64])
        vv = sb("vv", [128, GB, 256])
        QDb = sb("QDb", [128, 2, 2, 8, 64])
        QD = [QDb[:, i] for i in range(2)]
        E0 = [sb(f"E0{i}", [128, 8, 128]) for i in range(2)]
        PT0 = sb("PT0", [128, 8, 128])
        nm0 = [sb(f"nm0{i}", [128, 8]) for i in range(2)]
        sum0 = [sb(f"sum0{i}", [128, 8]) for i in range(2)]
        rs0 = [sb(f"rs0{i}", [128, 8]) for i in range(2)]
        tmpo = [sb(f"tmpo{i}", [128, 2, 64]) for i in range(2)]
        AO = sb("AO", [128, 2, GB, 64])
        aos = [sb(f"aos{i}", [128, 2, GB, 64], F32R) for i in range(2)]
        yy = sb("yy", [128, 2, 256])
        ysq = sb("ysq", [128, 256])
        ss = sb("ss", [128, 2])
        rr = sb("rr", [128, 2])
        ynT = [sb(f"ynT{i}", [128, 2, 256], F32R) for i in range(2)]
        hm = sb("hm", [128, 8, 256])
        gs = [sb(f"gs{i}", [128, 4, 256], F32R) for i in range(2)]
        X1 = [sb(f"X1{i}", [128, 256]) for i in range(4)]

        craw = sb("craw", [128, GB, 256])
        CH = [sb(f"CH{i}", [128, GB, 256], F32R) for i in range(2)]
        CL = [sb(f"CL{i}", [128, GB, 256], F32R) for i in range(2)]
        st6 = sb("st6", [128, 6])
        mv = sb("mv", [128, 2])
        mu = sb("mu", [128, 1])
        dd = sb("dd", [128, 1])
        ee = sb("ee", [128, 1])
        rstd = sb("rstd", [128, 1])
        aa = sb("aa", [128, 1])
        mb = sb("mb", [128, 1])
        bb = sb("bb", [128, 1])
        xnb = sb("xnb", [128, 2, 256])
        xnrm = [xnb[:, i] for i in range(2)]
        XS = [sb(f"XS{i}", [128, 256], F32R) for i in range(2)]
        QS = [sb(f"QS{i}", [128, 8, 256], F32R) for i in range(2)]
        VW = [sb(f"VW{i}", [128, 2, 512]) for i in range(2)]
        E1b = sb("E1b", [128, 4, 2, 256])
        E1 = [E1b[:, i] for i in range(4)]
        nm1 = [sb(f"nm1{i}", [128, 2]) for i in range(4)]
        sum1 = [sb(f"sum1{i}", [128, 2]) for i in range(4)]
        rs1 = [sb(f"rs1{i}", [128, 2]) for i in range(4)]
        PT1b = sb("PT1b", [128, 3, 2, 256])
        PT1 = [PT1b[:, i] for i in range(3)]

        sto = xnb[:, :, :]
        stk, stq = PT1b[:, 0:2], PT1b[:, 2]
        stw1 = hm[:, :, :].rearrange("p k n -> p (k n)").rearrange("p (k n) -> p k n", k=2)
        stage = QDb[:, :, :, :, :].rearrange("p a b c d -> p (a b c d)").rearrange("p (k n) -> p k n", k=8)
        l1w = E1b[0:64, :, :, :].rearrange("p w a n -> p w (a n)")
        y1 = [sb(f"y1{i}", [128, 256]) for i in range(2)]

        class Banks:

            def __init__(self, banks):
                self.idle = [(b, ()) for b in banks]

            def take(self):
                b, after = self.idle.pop(0)
                return b, after

            def give(self, b, *after):
                self.idle.append((b, after))

        BK = Banks(bank[0:7])
        OB = bank[7]

        def mm(out, lhsT, rhs, start, stop, *after, inc=False):
            return PE.do(lambda e: e.matmul(out, lhsT, rhs, start=start, stop=stop, skip_group_check=True), *after,
                         inc=inc)

        def three(out, a, b, start, stop, *after, inc=False):
            mm(out, a[0], b[0], start, False, *after)
            mm(out, a[0], b[1], False, False)
            return mm(out, a[1], b[0], False, stop, inc=inc)

        def f(ap):
            return ap.bitcast(F32)

        d_sm, d_q, d_kv, d_o, d_w1, d_w2, d_l1, d_mk = (sem(n) for n in
                                                        ("d_sm", "d_q", "d_kv", "d_o", "d_w1", "d_w2", "d_l1", "d_mk"))
        d_h, d_x, d_c, d_out = sem("d_h"), sem("d_x"), sem("d_c"), [sem("d_out0"), sem("d_out1")]
        t_small = SY.dma(lambda e: e.dma_start(small[:, :], sm_d), d_sm, 1)

        free_hraw, free_x, free_craw = (), (), ()
        loads = {}

        def load_group(g, after_h=(), after_x=(), after_c=()):
            th = SY.dma(lambda e: e.dma_start(hraw[:, :, :, :], hT[g].rearrange("p (k b t) -> p k b t", k=2, b=GB)),
                        d_h, g + 1, *after_h)
            tx = SY.dma(lambda e: e.dma_start(xnat[:, :, :], xn_d[g].rearrange("(u p) s -> p u s", p=128)),
                        d_x, g + 1, *after_x)
            src = ctx_d[g * GB:(g + 1) * GB].rearrange("b c s -> c b s")
            SY.dma(lambda e: e.dma_start(craw[0:64, :, :], src), d_c, 2 * g + 1, *after_c)
            tc = SY.dma(lambda e: e.dma_start(craw[64:128, :, :], src), d_c, 2 * g + 2)
            tk_ = SY.dma(lambda e: e.dma_start(mski[:, :, :], msk_d[:, g * GB:(g + 1) * GB, :]), d_mk, g + 1)
            loads[g] = (th, tx, tc, tk_)

        load_group(0)
        SY.dma(lambda e: e.dma_start(stk[:, 0, :, :], kvw_d[0].rearrange("(k p) n -> p k n", p=128)), d_kv, 1)
        t_kvw = SY.dma(lambda e: e.dma_start(stk[:, 1, :, :], kvw_d[1].rearrange("(k p) n -> p k n", p=128)), d_kv, 2)
        t_qw = SY.dma(lambda e: e.dma_start(stq[:, :, :], qw_d.rearrange("(k p) n -> p k n", p=128)), d_q, 1)
        t_ow = SY.dma(lambda e: e.dma_start(sto[:, :, :], ow_d.rearrange("(k p) n -> p k n", p=128)), d_o, 1)
        t_w1 = SY.dma(lambda e: e.dma_start(stw1[:, :, :], w1_d.rearrange("(k p) n -> p k n", p=128)), d_w1, 1)
        t_w2 = SY.dma(lambda e: e.dma_start(stage[:, :, :], w2_d.rearrange("(k p) n -> p k n", p=128)), d_w2, 1)
        t_l1 = SY.dma(lambda e: e.dma_start(l1w[:, :, :], l1_d.rearrange("w o n -> o w n")), d_l1, 1)

        def split(hi, lo, src, *after):
            t = VE.do(lambda e: e.tensor_copy(hi, src), *after)
            return VE.do(lambda e: e.tensor_tensor(lo, src, f(hi), ALU.subtract), t)

        t_ones = PO.do(lambda e: e.memset(onesb[:, :], 1.0))
        PO.do(lambda e: e.memset(mrow[0][:, :, :], 0.0))
        t_mz = PO.do(lambda e: e.memset(mrow[1][:, :, :], 0.0))
        t_hh0 = split(hh[0][:, :, :, :], hh[1][:, :, :, :], hraw[:, :, :, :], loads[0][0])
        t_wk = split(wk[0][:, :, :], wk[1][:, :, :], stk[:, 0, :, :], t_kvw)
        t_wv = split(wv[0][:, :, :], wv[1][:, :, :], stk[:, 1, :, :], t_kvw)
        t_wq = split(wq[0][:, :, :], wq[1][:, :, :], stq[:, :, :], t_qw)
        ready = {}

        def weights_late():
            ready["wo"] = split(wo[0][:, :, :], wo[1][:, :, :], sto[:, :, :], t_ow)
            b, fr = BK.take()
            vb = sm("vb")
            mm(b[:, 0:256], vb[:, 0:1].to_broadcast([128, 128]), sto[:, 0, :], True, False, t_ow, t_small, *fr)
            t = mm(b[:, 0:256], vb[:, 1:2].to_broadcast([128, 128]), sto[:, 1, :], False, True, inc=True)
            ready["obt"] = VE.do(lambda e: e.tensor_tensor(obt[:, :], b[:, 0:256], sm("ob"), ALU.add), t)
            BK.give(b, ready["obt"])
            yield
            pw = sm("pw")
            ts = [VE.do(lambda e, k=k: e.tensor_scalar(stw1[:, k, :], stw1[:, k, :], pw[:, k:k + 1], None, ALU.mult),
                        t_w1, t_small) for k in range(2)]
            ready["w1"] = split(w1[0][:, :, :], w1[1][:, :, :], stw1[:, :, :], *ts)
            ready["w2"] = split(w2[0][:, :, :], w2[1][:, :, :], stage[:, :, :], t_w2)
            yield
            W = l1w[:, :, :].rearrange("o w (h c) -> o w h c", h=8)

            def both(b, col, n, lhsT, rhs, start, stop, *after, inc=False):
                for a in range(0, 128, 64):
                    t = mm(b[a:a + 64, col:col + n], lhsT, rhs, start, stop, *after, inc=inc and a == 64)
                return t
            bM, f1 = BK.take()
            for h in range(8):
                tM = both(bM, h * 64, 64, W[:, 0, h, :], W[:, 1, h, :], h == 0, h == 7,
                        t_l1, *f1, inc=h == 7)
            bV, f2 = BK.take()
            for h in range(8):
                tV = both(bV, h * 64, 64, W[:, 2, h, :], W[:, 3, h, :], h == 0, h == 7, *f2, inc=h == 7)
            bU, f3 = BK.take()
            bq, bv = sm("bq"), sm("bv")
            for h in range(8):
                both(bU, h, 1, W[:, 1, h, :], bq[0:64, h:h + 1], h == 0, h == 7, t_small, *f3)
            for h in range(8):
                tU = both(bU, 8, 1, W[:, 3, h, :], bv[0:64, h:h + 1], False, h == 7, inc=h == 7)
            t = VE.do(lambda e: e.tensor_scalar(MM[0][:, :], bM[:, :], 0.125, None, ALU.mult), tM)
            ready["M"] = VE.do(lambda e: e.scalar_tensor_tensor(MM[1][:, :], bM[:, :], 0.125, f(MM[0][:, :]),
                                                                ALU.mult, ALU.subtract), t)
            BK.give(bM, ready["M"])
            t1 = VE.do(lambda e: e.tensor_copy(WS[:, :], bV[:, :]), tV)
            ready["V"] = VE.do(lambda e: e.tensor_tensor(WS[64:128, :], bV[64:128, :], f(WS[64:128, :]),
                                                         ALU.subtract), t1)
            BK.give(bV, ready["V"])
            VE.do(lambda e: e.tensor_scalar(uu[:, :], bU[:, 0:8], 0.125, None, ALU.mult), tU)
            ready["u"] = VE.do(lambda e: e.tensor_tensor(cbias[:, :], bU[:, 8:9], sm("bo"), ALU.add))
            BK.give(bU, ready["u"])
            yield

        st = dict(hh=t_hh0, hh_free=(), kT_free=(), qT_free=(), vv_free=(), ao_free=(), aos_free=(), xo_free=(),
                  yn_free=(), ynT_free=(), hm_free=(), gl_free=())
        st["gs_free", 0] = st["gs_free", 1] = None
        qd_free, e0_free, pt0_free = [None, None], [None, None], [None, None]
        x1_ready, x1_free = {}, [(), (), (), ()]
        c_ready, c_free = {}, [(), ()]

        def layer0(g):
            th, tx, tc, tkm = loads[g]
            t_mrow = VE.do(lambda e: e.tensor_scalar(mrow[g % 2][0:1, :, 0:64], mski[:, :, :], 0.0, NEG, ALU.is_equal,
                                                     ALU.mult), tkm, t_mz, qd_free[(GB - 1) % 2])
            if g == 0:
                thh = st["hh"]
            else:
                thh = split(hh[0][:, :, :, :], hh[1][:, :, :, :], hraw[:, :, :, :], th, *st["hh_free"])
            t_xo = None
            yield
            yield
            tk = []
            for m in range(2):
                b, fr = BK.take()
                for kt in range(2):
                    a = [w[:, kt, m * 128:(m + 1) * 128] for w in wk]
                    t = three(b[:, :], a, [x[:, kt, :, :] for x in hh], kt == 0, kt == 1, thh, t_wk, *fr, inc=kt == 1)
                yield
                kb = sm("kb")
                tk.append(SC.do(lambda e, m=m, b=b: e.activation(kT[:, m, :, :], b[:, :].rearrange(
                    "p (b t) -> p b t", b=GB), ACT.Identity, bias=kb[:, m:m + 1], scale=1.0), t, t_small,
                    *st["kT_free"]))
                BK.give(b, tk[-1])
                yield
            b, fr = BK.take()
            for m in range(2):
                for kt in range(2):
                    a = [w[:, kt, m * 128:(m + 1) * 128] for w in wq]
                    t = three(b[:, m * 256:(m + 1) * 256], a, [x[:, kt, :, 64:128] for x in hh],
                              m == 0 and kt == 0, kt == 1, t_wq, *fr, inc=kt == 1)
            yield
            for m in range(2):
                qb = sm("qb")
                tq = VE.do(lambda e, m=m, b=b: e.tensor_scalar(
                    qT[:, m, :, :], b[:, m * 256:(m + 1) * 256].rearrange("p (b t) -> p b t", b=GB),
                    qb[:, m:m + 1], 0.0625, ALU.add, ALU.mult), t, t_small, *st["qT_free"])
            BK.give(b, tq)
            yield
            tv = []
            for u in range(2):
                b, fr = BK.take()
                for i in range(2):
                    for kt in range(2):
                        a = [x[:, kt, 2 * u + i, :] for x in hh]
                        t = three(b[:, i * 256:(i + 1) * 256], a, [w[:, kt, :] for w in wv],
                                  i == 0 and kt == 0, kt == 1, t_wv, *fr, inc=i == 1 and kt == 1)
                tlast = t
                yield
                tv.append(SC.do(lambda e, u=u, b=b: e.copy(
                    vv[:, 2 * u:2 * u + 2, :], b[:, :].rearrange("p (b n) -> p b n", b=2)), t, *st["vv_free"]))
                BK.give(b, tv[-1])
                yield
            st["hh_free"] = (tlast,)
            if g == 0:
                yield from weights_late()
            t_xo = PO.do(lambda e: e.tensor_tensor(xo[:, :, :], xnat[:, :, :], obt[:, :].unsqueeze(1).to_broadcast(
                [128, 2, 256]), ALU.add), tx, ready["obt"], *st["xo_free"])
            t_xb = PO.do(lambda e: e.tensor_tensor(xnat[:, :, :], xnat[:, :, :], sm("b2").unsqueeze(1).to_broadcast(
                [128, 2, 256]), ALU.add), t_xo)
            yield
            tAO, keep = [], {}

            def at_q(b, m):
                r = b % 2
                keep["qd", b] = PO.do(lambda e: e.tensor_tensor(
                    QD[r][:, m, :, :], qT[:, m, b, :].unsqueeze(1).to_broadcast([128, 8, 64]),
                    sm("hm").unsqueeze(2).to_broadcast([128, 8, 64]), ALU.mult), tq, qd_free[r], ready["w2"])

            def s_mm(b, m):
                r = b % 2
                pb, fr = BK.take()
                mm(pb[:, :], onesb[:, :], mrow[g % 2][:, b, :].unsqueeze(1).to_broadcast([128, 4, 128]), True, False,
                   t_mrow, t_ones, keep["qd", b], tk[m], *fr)
                for j in range(4):
                    t = mm(pb[:, j * 128:(j + 1) * 128], QD[r][:, m, 2 * j:2 * j + 2, :], kT[:, m, b, :],
                           False, j == 3, inc=j == 3)
                if m == 1:
                    qd_free[r] = t
                keep["s", b] = (pb, t)

            def s_max(b, m):
                r = b % 2
                pb, t = keep["s", b]
                keep["m", b] = VE.do(lambda e: e.tensor_reduce(
                    nm0[r][:, 4 * m:4 * m + 4], pb[:, :].rearrange("p (j t) -> p j t", j=4), AX.X, ALU.max,
                    negate=True), t, e0_free[r])

            def s_exp(b, m):
                r = b % 2
                pb, t = keep["s", b]
                for j in range(4):
                    jj = 4 * m + j
                    t2 = SC.do(lambda e, j=j, jj=jj: e.activation(
                        E0[r][:, jj, :], pb[:, j * 128:(j + 1) * 128], ACT.Exp, bias=nm0[r][:, jj:jj + 1],
                        scale=1.0, accum_out=sum0[r][:, jj:jj + 1]), keep["m", b], e0_free[r])
                BK.give(pb, t2)
                keep["e", b] = t2

            def at_n(b, m):
                r, c = b % 2, slice(4 * m, 4 * m + 4)
                t = VE.do(lambda e: e.reciprocal(rs0[r][:, c], sum0[r][:, c]), keep["e", b])
                keep["n", b] = PO.do(lambda e: e.tensor_tensor(
                    E0[r][:, c, :], E0[r][:, c, :], rs0[r][:, c].unsqueeze(2).to_broadcast([128, 4, 128]),
                    ALU.mult), t)

            def t_mm(b, m):
                r = b % 2
                pb, fr = BK.take()
                for j in range(4):
                    t = PE.do(lambda e, j=j: e.transpose(pb[:, j * 128:(j + 1) * 128], E0[r][:, 4 * m + j, :],
                                                         sm("ident")), keep["n", b], *fr, inc=j == 3)
                if m == 1:
                    e0_free[r] = t
                keep["tp", b] = (pb, t)

            def t_ev(b, m):
                pb, t = keep["tp", b]
                tt = SC.do(lambda e: e.copy(PT0[:, 4 * m:4 * m + 4, :], pb[:, :].rearrange(
                    "p (j t) -> p j t", j=4)), t, pt0_free[0])
                BK.give(pb, tt)
                keep["t", b] = tt

            def v_mm(b):
                pb, fr = BK.take()
                for m in range(2):
                    for j in range(4):
                        t = mm(pb[32 * j:32 * j + 32, m * 128:(m + 1) * 128],
                               vv[:, b, 128 * m + 32 * j:128 * m + 32 * j + 32], PT0[:, 4 * m + j, :],
                               m == 0, m == 1, tv[b // 2], keep["t", b], *fr, inc=m == 1 and j == 3)
                pt0_free[0] = t
                keep["o", b] = (pb, t)

            def v_ev(b, which):
                r = b % 2
                pb, t = keep["o", b]
                o = pb[:, 0:256].rearrange("p (m h q) -> p m h q", m=2, h=2)
                par = sm("par")
                if which == 0:
                    keep["o2", b] = SC.do(lambda e: e.activation(tmpo[r][:, :, :], o[:, :, 0, :], ACT.Copy, bias=0.0,
                                                                 scale=par[:, 0:1]), t, keep.get(("ao", b - 2)))
                    return
                t3 = VE.do(lambda e: e.scalar_tensor_tensor(AO[:, :, b, :], o[:, :, 1, :], par[:, 1:2],
                                                            tmpo[r][:, :, :], ALU.mult, ALU.add), keep["o2", b],
                           *st["ao_free"])
                BK.give(pb, t3)
                keep["ao", b] = t3

            micro = {0: lambda b: at_q(b, 0), 1: lambda b: at_q(b, 1), 5: lambda b: s_mm(b, 0),
                     6: lambda b: s_max(b, 0), 7: lambda b: s_exp(b, 0), 8: lambda b: (at_n(b, 0), s_mm(b, 1)),
                     9: lambda b: s_max(b, 1), 10: lambda b: s_exp(b, 1), 11: lambda b: at_n(b, 1),
                     15: lambda b: t_mm(b, 0), 16: lambda b: t_ev(b, 0), 17: lambda b: t_mm(b, 1),
                     18: lambda b: t_ev(b, 1), 19: lambda b: v_mm(b), 20: lambda b: v_ev(b, 0),
                     21: lambda b: v_ev(b, 1)}
            OFF = 9
            for i in range(OFF * (GB - 1) + max(micro) + 1):
                for b in range(GB):
                    if i - OFF * b in micro:
                        micro[i - OFF * b](b)
                yield
            st["qT_free"] = (keep["qd", GB - 1],)
            st["kT_free"] = (qd_free[(GB - 1) % 2],)
            st["vv_free"] = (pt0_free[0],)
            t = split(aos[0][:, :, :, :], aos[1][:, :, :, :], AO[:, :, :, :], keep["ao", GB - 1], *st["aos_free"])
            st["ao_free"] = (t,)
            yield
            yield
            pb, fr = BK.take()
            for u in range(2):
                for kt in range(2):
                    a = [x[:, kt, 2 * u:2 * u + 2, :] for x in aos]
                    t1 = three(pb[:, u * 256:(u + 1) * 256], a, [w[:, kt, :] for w in wo], u == 0 and kt == 0,
                               kt == 1, t, ready["wo"], *fr, inc=u == 1 and kt == 1)
            st["aos_free"] = (t1,)
            yield
            t = VE.do(lambda e, pb=pb: e.tensor_tensor(yy[:, :, :], pb[:, :].rearrange("p (u n) -> p u n", u=2), xo[:, :, :],
                                                ALU.add), t1, t_xo)
            BK.give(pb, t)
            st["xo_free"] = (t,)
            for u in range(2):
                tt = VE.do(lambda e, u=u: e.tensor_tensor_reduce(
                    ysq[:, :], yy[:, u, :], yy[:, u, :], 1.0 / 256, 0.0, ALU.mult, ALU.add, ss[:, u:u + 1]), t)
                t = tt
            t = VE.do(lambda e: e.tensor_scalar(rr[:, :], ss[:, :], 1e-6, None, ALU.add), t)
            t = PO.do(lambda e: e.tensor_tensor(rr[:, :], rr[:, :], sm("mh"), ALU.pow), t)
            yield
            for u in range(2):
                tn = VE.do(lambda e, u=u: e.tensor_scalar(yy[:, u, :], yy[:, u, :], rr[:, u:u + 1], None, ALU.mult),
                           t, *st["yn_free"])
            yield
            yield
            pb, fr = BK.take()
            for kt in range(2):
                for u in range(2):
                    t = PE.do(lambda e, kt=kt, u=u, pb=pb: e.transpose(pb[:, kt * 256 + u * 128:kt * 256 + u * 128 + 128],
                                                                yy[:, u, kt * 128:(kt + 1) * 128], sm("ident")),
                              tn, *fr, inc=kt == 1 and u == 1)
            st["yn_free"] = (t,)
            yield
            src = pb[:, :].rearrange("p (k t) -> p k t", k=2)
            t1 = SC.do(lambda e: e.copy(ynT[0][:, :, :], src), t, *st["ynT_free"])
            tT = VE.do(lambda e: e.tensor_tensor(ynT[1][:, :, :], src, f(ynT[0][:, :, :]), ALU.subtract), t1)
            BK.give(pb, tT)
            yield
            yield
            b1 = sm("b1")
            for c in range(4):
                pb, fr = BK.take()
                for i in range(2):
                    m = 2 * c + i
                    for kt in range(2):
                        a = [w[:, kt, m * 128:(m + 1) * 128] for w in w1]
                        t = three(pb[:, i * 256:(i + 1) * 256], a, [x[:, kt, :] for x in ynT], i == 0 and kt == 0,
                                  kt == 1, tT, ready["w1"], *fr, inc=i == 1 and kt == 1)
                st["ynT_free"] = (t,)
                yield
                th_ = VE.do(lambda e, c=c, pb=pb: e.tensor_tensor(
                    hm[:, 2 * c:2 * c + 2, :], pb[:, :].rearrange("p (i t) -> p i t", i=2),
                    b1[:, 2 * c:2 * c + 2].unsqueeze(2).to_broadcast([128, 2, 256]), ALU.add), t, *st["hm_free"])
                BK.give(pb, th_)
                yield
            yield
            yield
            tg = SC.do(lambda e: e.activation(hm[:, :, :], hm[:, :, :], ACT.Gelu_apprx_tanh), th_, *st["gl_free"])
            yield
            pb, fr = BK.take()
            gs_ready = {}
            for c in range(6):
                if c >= 2:
                    d = c - 2
                    for u in range(2):
                        for kt in range(2 * d, 2 * d + 2):
                            a = [x[:, kt % 4, u * 128:(u + 1) * 128] for x in gs]
                            t = three(pb[:, u * 256:(u + 1) * 256], a, [w[:, kt, :] for w in w2], kt == 0 and u == 0,
                                      kt == 7, gs_ready[d], ready["w2"], *fr, inc=kt % 2 == 1)
                    st["gs_free", d % 2] = t
                    yield
                if c < 4:
                    z = slice(2 * (c % 2), 2 * (c % 2) + 2)
                    t = VE.do(lambda e, c=c, z=z: e.tensor_copy(gs[0][:, z, :], hm[:, 2 * c:2 * c + 2, :]), tg,
                              st["gs_free", c % 2])
                    gs_ready[c] = PO.do(lambda e, c=c, z=z: e.tensor_tensor(
                        gs[1][:, z, :], hm[:, 2 * c:2 * c + 2, :], f(gs[0][:, z, :]), ALU.subtract), t)
                    yield
            tgs = gs_ready[3]
            yield
            st["hm_free"] = (tgs,)
            for u in range(2):
                p = 2 * g + u
                x1_ready[p] = VE.do(lambda e, u=u, p=p: e.tensor_tensor(
                    X1[p % 4][:, :], pb[:, u * 256:(u + 1) * 256], xnat[:, u, :], ALU.add), t, t_xb, *x1_free[p % 4])
            BK.give(pb, x1_ready[2 * g + 1])
            cs = g % 2
            t1 = VE.do(lambda e: e.tensor_copy(CH[cs][:, :, :], craw[:, :, :]), tc, *c_free[cs])
            c_ready[g] = PO.do(lambda e: e.tensor_tensor(CL[cs][:, :, :], craw[:, :, :], f(CH[cs][:, :, :]),
                                                         ALU.subtract), t1, *c_free[cs])
            yield
            if g + 1 < NG:
                load_group(g + 1, (thh,), (x1_ready[2 * g + 1],), (c_ready[g], t_mrow))
            yield

        xn_ready, qs_ready, vw_ready = {}, {}, {}
        xnrm_free, xs_free, qs_free, vw_free = [(), ()], [(), ()], [(), ()], [(), ()]

        def norm_pair(p):
            x = X1[p % 4]
            t = VE.do(lambda e: e.bn_stats(st6[:, :], x[:, :]), x1_ready[p])
            tm = VE.do(lambda e: e.bn_aggr(mv[:, :], st6[:, :]), t)
            yield
            pb, fr = BK.take()
            t = mm(pb[:, 0:1], sm("avg"), mv[:, 0:1], True, True, tm, t_small, *fr, inc=True)
            yield
            tmu = VE.do(lambda e: e.tensor_copy(mu[:, :], pb[:, 0:1]), t)
            t = VE.do(lambda e: e.tensor_tensor(dd[:, :], mv[:, 0:1], mu[:, :], ALU.subtract), tmu)
            t = VE.do(lambda e: e.scalar_tensor_tensor(ee[:, :], dd[:, :], dd[:, 0:1], mv[:, 1:2], ALU.mult, ALU.add),
                      t)
            yield
            t = mm(pb[:, 2:3], sm("avg"), ee[:, :], True, True, t, inc=True)
            yield
            t = VE.do(lambda e: e.tensor_scalar(rstd[:, :], pb[:, 2:3], 1e-5, None, ALU.add), t)
            BK.give(pb, t)
            t = PO.do(lambda e: e.tensor_tensor(rstd[:, :], rstd[:, :], sm("mh")[:, 0:1], ALU.pow), t)
            yield
            t = VE.do(lambda e: e.tensor_tensor(aa[:, :], rstd[:, :], sm("gamma"), ALU.mult), t)
            t = VE.do(lambda e: e.tensor_tensor(mb[:, :], mu[:, :], aa[:, :], ALU.mult), t)
            t = VE.do(lambda e: e.tensor_tensor(bb[:, :], sm("beta"), mb[:, :], ALU.subtract), t)
            xn_ready[p] = VE.do(lambda e: e.tensor_scalar(xnrm[p % 2][:, :], x[:, :], aa[:, 0:1], bb[:, 0:1],
                                                          ALU.mult, ALU.add), t, *xnrm_free[p % 2])
            yield

        def prep(n):
            p, o, s, g, bg = n // 2, 64 * (n % 2), n % 2, n // GB, n % GB
            if n % 2 == 0:
                yield from norm_pair(p)
            q = 64 - o
            xr = xnrm[p % 2]
            yield
            t = SC.do(lambda e: e.copy(XS[s][o:o + 64, :], xr[o:o + 64, :]), xn_ready[p], *xs_free[s])
            yield
            txs = VE.do(lambda e: e.tensor_tensor(XS[s][q:q + 64, :], xr[o:o + 64, :], f(XS[s][o:o + 64, :]),
                                                  ALU.subtract), t)
            if n % 2 == 1:
                xnrm_free[p % 2] = (txs,)
            yield
            yield
            ch, cl = CH[g % 2], CL[g % 2]
            for c in range(2):
                pb, fr = BK.take()
                for i in range(2):
                    pr = 2 * c + i
                    sl = pb[:, i * 256:(i + 1) * 256]
                    mm(sl, MM[0][:, pr * 128:(pr + 1) * 128], XS[s][:, :], i == 0, False, txs, ready["M"],
                       ready["u"], *fr)
                    t = mm(sl, MM[1][:, pr * 128:(pr + 1) * 128], XS[s][:, :], False, True, inc=i == 1)
                tlast = t
                yield
                yield
                where = [(4 * c + j, 64 * (j % 2), pb[64 * (j % 2):64 * (j % 2) + 64, 256 * (j // 2):256 * (j // 2) + 256])
                         for j in range(4)]
                for d in range(2):
                    for h, a, sl in where[2 * d:2 * d + 2]:
                        th = SC.do(lambda e, h=h, a=a, sl=sl: e.activation(
                            QS[s][a:a + 64, h, :], sl, ACT.Identity, bias=uu[a:a + 64, h:h + 1], scale=1.0),
                            t, *qs_free[s])
                    yield
                for d in range(2):
                    for h, a, sl in where[2 * d:2 * d + 2]:
                        z = 64 - a
                        tl = VE.do(lambda e, h=h, a=a, z=z, sl=sl: e.scalar_tensor_tensor(
                            QS[s][z:z + 64, h, :], sl, uu[a:a + 64, h:h + 1], f(QS[s][a:a + 64, h, :]), ALU.add,
                            ALU.subtract), th, *qs_free[s])
                        qs_ready[n, h] = tl
                    yield
                BK.give(pb, tl)
                yield
            xs_free[s] = (tlast,)
            while n >= 2 and ("v", n - 2) not in hs:
                yield
            tv = []
            for j in range(2):
                pb, fr = BK.take()
                mm(pb[:, :], ch[:, bg, j * 128:(j + 1) * 128], WS[:, :], True, False, ready["V"], c_ready[g], *fr)
                t = mm(pb[:, :], cl[:, bg, j * 128:(j + 1) * 128], WS[:, :], False, True, inc=True)
                yield
                E = (SC, VE)[j]
                tv.append(E.do((lambda e, pb=pb: e.copy(VW[s][:, 0, :], pb[:, :])) if j == 0 else
                               (lambda e, pb=pb: e.tensor_copy(VW[s][:, 1, :], pb[:, :])), t, *vw_free[s]))
                BK.give(pb, tv[-1])
            vw_ready[n] = tv
            yield

        e1_free, pt1_free, hs = [None] * 4, [None] * 3, {}
        o_free, y1_free, yo_free = [None, None], [None, None], [None, None]

        def stage_s(t_):
            n, h = divmod(t_, 8)
            s, g, bg, r = n % 2, n // GB, n % GB, t_ % 4
            pb, fr = BK.take()
            for i in range(2):
                a = QS[s][:, h, i * 128:(i + 1) * 128]
                mm(pb[:, i * 256:(i + 1) * 256], a, CH[g % 2][:, bg, :], i == 0, False, qs_ready[n, h], *fr)
                t = mm(pb[:, i * 256:(i + 1) * 256], a, CL[g % 2][:, bg, :], False, True, inc=i == 1)
            if h == 7:
                qs_free[s] = (t,)
                if bg == GB - 1:
                    hs["c", g] = t
            hs["s", t_] = (pb, t)

        def stage_x(t_):
            r = t_ % 4
            pb, t = hs["s", t_]
            hs["m", t_] = VE.do(lambda e: e.tensor_reduce(nm1[r][:, :], pb[:, :].rearrange("p (i t) -> p i t", i=2), AX.X,
                                                ALU.max, negate=True), t, e1_free[r])

        def stage_e(t_):
            r = t_ % 4
            pb, t = hs["s", t_]
            for i in range(2):
                t2 = SC.do(lambda e, i=i: e.activation(E1[r][:, i, :], pb[:, i * 256:(i + 1) * 256], ACT.Exp,
                                                       bias=nm1[r][:, i:i + 1], scale=1.0,
                                                       accum_out=sum1[r][:, i:i + 1]), hs["m", t_], e1_free[r])
            BK.give(pb, t2)
            hs["e", t_] = t2

        def stage_n(t_):
            r = t_ % 4
            t = VE.do(lambda e: e.reciprocal(rs1[r][:, :], sum1[r][:, :]), hs["e", t_])
            hs["n", t_] = PO.do(lambda e: e.tensor_tensor(
                E1[r][:, :, :], E1[r][:, :, :], rs1[r][:, :].unsqueeze(2).to_broadcast([128, 2, 256]), ALU.mult), t)

        def stage_t(t_):
            r = t_ % 4
            pb, fr = BK.take()
            for j in range(2):
                for i in range(2):
                    t = PE.do(lambda e, i=i, j=j: e.transpose(
                        pb[:, j * 256 + i * 128:j * 256 + i * 128 + 128], E1[r][:, i, j * 128:(j + 1) * 128],
                        sm("ident")), hs["n", t_], *fr, inc=i == 1 and j == 1)
            e1_free[r] = t
            hs["tp", t_] = (pb, t)

        def stage_u(t_):
            r3 = t_ % 3
            pb, t = hs["tp", t_]
            src = pb[:, :].rearrange("p (j t) -> p j t", j=2)
            if t_ % 4 == 3:
                t2 = SC.do(lambda e: e.copy(PT1[r3][:, :, :], src), t, pt1_free[r3])
            else:
                t2 = VE.do(lambda e: e.tensor_copy(PT1[r3][:, :, :], src), t, pt1_free[r3])
            BK.give(pb, t2)
            hs["t", t_] = t2

        def stage_v(t_):
            n, h = divmod(t_, 8)
            r3, s, c = t_ % 3, n % 2, 64 * (h % 2)
            o = OB[c:c + 64, s * 256:(s + 1) * 256]
            for j in range(2):
                t = mm(o, VW[s][:, j, h * 64:(h + 1) * 64], PT1[r3][:, j, :], h < 2 and j == 0, h >= 6 and j == 1,
                       hs["t", t_], vw_ready[n][j], o_free[0], inc=j == 1)
            pt1_free[r3] = t
            if h == 7:
                vw_free[s] = (t,)
                hs["v", n] = t

        def finish(n):
            p, a, s = n // 2, 64 * (n % 2), n % 2
            x = X1[p % 4]
            o = OB[:, s * 256:(s + 1) * 256]
            t = VE.do(lambda e: e.scalar_tensor_tensor(y1[p % 2][a:a + 64, :], o[a:a + 64, :], cbias[a:a + 64, 0:1],
                                                       x[a:a + 64, :], ALU.add, ALU.add), hs["v", n], yo_free[p % 2],
                      ready["u"])
            z = 64 - a
            t = VE.do(lambda e: e.tensor_tensor(y1[p % 2][a:a + 64, :], o[z:z + 64, :], y1[p % 2][a:a + 64, :],
                                                ALU.add), t, None)
            o_free[0] = t
            if s == 1:
                x1_free[p % 4] = (t,)
                yo_free[p % 2] = SY.dma(lambda e: e.dma_start(out_d[2 * p:2 * p + 2].rearrange("b c s -> (b c) s"),
                                                              y1[p % 2][:, :]), d_out[p % 2], p // 2 + 1, t)

        CH0, CH1, LE, LN, LT, LU, LV = CFG
        left0, left1 = [], []
        cnt=0
        for _ in layer0(0):
            cnt+=1
        for _ in prep(0):
            pass
        T = NB * 8
        stages = [(0, stage_s), (1, stage_x), (LE, stage_e), (LN, stage_n), (LT, stage_t), (LU, stage_u), (LV, stage_v)]
        bg0, bg1, n0, done0, done1 = None, None, 100, 0, 0
        for t_ in range(T + LV):
            n, h = divmod(t_, 8)
            if t_ < T and h == 0 and n % GB == 0:
                if n // GB + 1 < NG:
                    if n // GB >= 1:
                        c_free[(n // GB + 1) % 2] = (hs["c", n // GB - 1],)
                    bg0, done0 = layer0(n // GB + 1), 0
            if t_ < T and h == 7 and n + 1 < NB:
                pass
            for i, (lag, step) in enumerate(stages):
                if 0 <= t_ - lag < T:
                    step(t_ - lag)
                    if step is stage_v and (t_ - lag) % 8 == 7:
                        finish((t_ - lag) // 8)
                if bg0 is not None:
                    at = 7 * (8 * (n % GB) + h) + i
                    while done0 < CH0 * (at + 1) / 168:
                        done0 += 1
                        next(bg0, None)
                if bg1 is not None and t_ < T:
                    while done1 < CH1 * (7 * h + i - 7) / 42:
                        done1 += 1
                        next(bg1, None)
                if step is stage_v and t_ < T and n + 1 < NB and h == 0:
                    bg1, done1 = prep(n + 1), 0
            if t_ < T and h == 7:
                if bg1 is not None:
                    for _ in bg1:
                        left1.append(1)
                    bg1 = None
                if bg0 is not None and n % GB == GB - 2:
                    for _ in bg0:
                        left0.append(1)
                    bg0 = None

        pass
        SY.do(None, (d_out[0], 16 * (NB // 4)), (d_out[1], 16 * (NB // 4)), inc=False)

        block = es.enter_context(nc.Block())

        @block.sync
        def _(e):
            SY.play(e)

        @block.tensor
        def _(e):
            PE.play(e)

        @block.vector
        def _(e):
            VE.play(e)

        @block.scalar
        def _(e):
            SC.play(e)

        @block.gpsimd
        def _(e):
            PO.play(e)


def kernel(x, ctx_2048, mask_BxS2_ik0, L0_xattn_q_w, L0_xattn_q_b, L0_xattn_kv_w, L0_xattn_kv_b, L0_xattn_out_w,
           L0_xattn_out_b, L0_xattn_postnorm_w, L0_xattn_mlp_w1, L0_xattn_mlp_b1, L0_xattn_mlp_w2, L0_xattn_mlp_b2,
           L1_xattn_gamma, L1_xattn_beta, L1_xattn_Wq, L1_xattn_bq, L1_xattn_Wkv, L1_xattn_bkv, L1_xattn_Wo,
           L1_xattn_bo):
    import numpy as np
    import concourse.bacc as bacc
    from concourse.bass_utils import run_bass_kernel_spmd

    asc = np.ascontiguousarray
    x = np.asarray(x)
    ctx = np.asarray(ctx_2048)
    h = np.concatenate([ctx, x], axis=1).reshape(NG, GB, 128, 2, 128)
    hT = asc(h.transpose(0, 4, 3, 1, 2)).reshape(NG, 128, 2 * GB * 128)
    kvw = asc(np.asarray(L0_xattn_kv_w).reshape(256, 256, 2).transpose(2, 0, 1))
    kvb = np.asarray(L0_xattn_kv_b).reshape(256, 2)
    wkv = np.asarray(L1_xattn_Wkv).reshape(2, 8, 64, 64)

    def heads(w):
        return np.asarray(w).reshape(8, 64, 64).transpose(1, 0, 2).reshape(64, 512)
    l1 = asc(np.stack([heads(L1_xattn_Wq), heads(wkv[0]), heads(wkv[1]), heads(np.asarray(L1_xattn_Wo).T)]))

    small = np.zeros((128, SMW), np.float32)

    def put(name, a):
        o, n = SM[name]
        small[:, o:o + n] = a
    put("qb", np.asarray(L0_xattn_q_b).reshape(2, 128).T)
    put("kb", kvb[:, 0].reshape(2, 128).T)
    put("vb", kvb[:, 1].reshape(2, 128).T)
    put("b1", np.asarray(L0_xattn_mlp_b1).reshape(8, 128).T)
    put("pw", np.asarray(L0_xattn_postnorm_w).reshape(2, 128).T)

    def twice(a):
        a = np.asarray(a)
        return np.concatenate([a, a], axis=0)
    put("gamma", twice(L1_xattn_gamma)[:, None])
    put("beta", twice(L1_xattn_beta)[:, None])
    put("bo", twice(L1_xattn_bo)[:, None])
    put("bq", twice(np.asarray(L1_xattn_bq).reshape(8, 64).T))
    bkv = np.asarray(L1_xattn_bkv).reshape(2, 8, 64)
    put("bk", twice(bkv[0].T))
    put("bv", twice(bkv[1].T))
    p = np.arange(128)
    put("par", ((p[:, None] // 16) % 2 == np.arange(2)[None, :]).astype(np.float32))
    put("hm", (p[:, None] // 16 == np.arange(8)[None, :]).astype(np.float32))
    put("ob", np.asarray(L0_xattn_out_b)[None, :])
    put("b2", np.asarray(L0_xattn_mlp_b2)[None, :])
    put("mh", np.float32(-0.5))
    put("ident", np.eye(128, dtype=np.float32))
    put("avg", np.where(p[:, None] // 64 == p[None, :] // 64, np.float32(1 / 64), np.float32(0)))

    arrays = {
        "hT": hT, "xn": asc(x.reshape(NG, 256, 256)), "ctx": asc(ctx),
        "msk": asc(np.asarray(mask_BxS2_ik0)).reshape(1, NB, 64), "qw": asc(L0_xattn_q_w), "kvw": kvw,
        "ow": asc(L0_xattn_out_w), "w1": asc(L0_xattn_mlp_w1), "w2": asc(L0_xattn_mlp_w2), "l1": l1, "sm": small,
    }
    nc = bacc.Bacc("TRN2", target_bir_lowering=False, num_devices=1)
    args = [nc.dram_tensor(f"in_{k}", a.shape, mybir.dt.from_np(a.dtype), kind="ExternalInput").ap()
            for k, a in arrays.items()]
    out = nc.dram_tensor("out_0", (NB, 64, 256), F32, kind="ExternalOutput").ap()
    build(nc, *args, out)
    r = run_bass_kernel_spmd(nc, [{f"in_{k}": a for k, a in arrays.items()}], core_ids=[0])
    return r.results[0]["out_0"]
```

```python
from contextlib import ExitStack

import concourse.bass as bass
from concourse import mybir

F32 = mybir.dt.float32
F32R = mybir.dt.float32r
BF16 = mybir.dt.bfloat16
I32 = mybir.dt.int32
ALU = mybir.AluOpType
ACT = mybir.ActivationFunctionType
AX = mybir.AxisListType

NB = 32
GB = 4
NG = NB // GB
NEG = -1.0e30
OFF, OFF0 = 8, 5
CUT = 24
ORD = (2, 1, 4, 3, 0, 5, 6)
MIC = (0, 2, 5, 6, 7, 8, 8, 9, 10, 13, 16, 17, 19, 21, 23, 24, 24)
CHA = 68
LX = 1
PRI = (0, 1, 2)
L1AT = 2
EV = (1, 1, 0, 1, 0, 0, 0, 1)
RES = 1
WA = 1.3
BEG = 0
LATE = 2
HEAD = (20, 25, 25, 42, 42, 5, 13)
UA = (76, 300)
SH = (6, 1, 0, 4, 2, 6, 10)
MIC0 = (0, 1, 3, 4, 5, 6, 7, 7, 8, 10, 11, 12, 13, 14, 15, 16, 17)
SP = (2, 1, 1, 0, 2, 1, 1, 1, 1, 2, 1, 1, 2, 1, 2, 0, 3, 2, 1, 4, 2, 0, 0, 1, 2, 1, 0, 2, 2, 1, 2, 2, 2, 1, 1, 1, 1, 5)
CFG = (96, 27, 2, 3, 5, 6, 7)

SM = dict(qb=(0, 2), kb=(2, 2), vb=(4, 2), b1=(6, 8), pw=(14, 2), gamma=(16, 1), beta=(17, 1),
          bo=(18, 1), bq=(19, 8), bv=(27, 8), par=(35, 2), hm=(37, 8), ob=(45, 256), b2=(301, 256),
          ident=(557, 128), avg=(685, 128), mh=(813, 2))
SMW = 815


class Engine:

    def __init__(self, sem):
        self.sem = sem
        self.n = 0
        self.todo = []
        self.seen = {}

    def do(self, emit, *after, inc=True):
        waits = []
        for t in after:
            if t is None:
                continue
            sem, v = t
            if self.seen.get(id(sem), 0) < v:
                self.seen[id(sem)] = v
                waits.append((sem, v))
        if inc:
            self.n += 1
        self.todo.append((waits, emit, self.sem if inc else None, 1))
        return (self.sem, self.n)

    def dma(self, emit, sem, count, *after):
        self.do(emit, *after, inc=False)
        waits, emit, _, _ = self.todo[-1]
        self.todo[-1] = (waits, emit, sem, 16)
        return (sem, 16 * count)

    def play(self, eng):
        for waits, emit, sem, k in self.todo:
            for s, v in waits:
                eng.wait_ge(s, v)
            if emit is None:
                continue
            ins = emit(eng)
            if sem is not None:
                ins.then_inc(sem, k)


def build(nc, hT, xn_d, ctx_d, msk_d, qw_d, kvw_d, ow_d, w1_d, w2_d, l1_d, sm_d, out_d):
    with ExitStack() as es:
        def sb(name, shape, dt=F32):
            return es.enter_context(nc.sbuf_tensor(name, shape, dt))

        def sem(name):
            return es.enter_context(nc.semaphore(name))

        bank = [es.enter_context(nc.psum_tensor(f"bank{i}", [128, 512], F32)) for i in range(8)]

        PE, VE, SC, PO, SY = (Engine(sem(n)) for n in ("s_pe", "s_ve", "s_sc", "s_po", "s_sy"))

        small = sb("small", [128, SMW])

        def sm(name):
            a, n = SM[name]
            return small[:, a:a + n]

        wq = [sb(f"wq{i}", [128, 2, 256], F32R) for i in range(2)]
        wk = [sb(f"wk{i}", [128, 2, 256], F32R) for i in range(2)]
        wv = [sb(f"wv{i}", [128, 2, 256], F32R) for i in range(2)]
        wo = [sb(f"wo{i}", [128, 2, 256], F32R) for i in range(2)]
        w1 = [sb(f"w1{i}", [128, 2, 1024], F32R) for i in range(2)]
        w2 = [sb(f"w2{i}", [128, 8, 256], F32R) for i in range(2)]
        MM = [sb(f"MM{i}", [128, 512], F32R) for i in range(2)]
        WS = sb("WS", [128, 512], F32R)
        uu = sb("uu", [128, 8])
        cbias = sb("cbias", [128, 1])
        obt = sb("obt", [128, 256])
        mski = sb("mski", [1, GB, 64], I32)
        mrow = [sb(f"mrow{i}", [128, GB, 64], BF16) for i in range(2)]
        onesb = sb("onesb", [128, 128], BF16)

        hraw = sb("hraw", [128, 2, GB, 128])
        hh = [sb(f"hh{i}", [128, 2, GB, 128], F32R) for i in range(2)]
        xnat = sb("xnat", [128, 2, 256])
        xo = sb("xo", [128, 2, 256])
        kT = sb("kT", [128, 2, GB, 128])
        qT = sb("qT", [128, 2, GB, 64])
        vv = sb("vv", [128, GB, 256])
        QDb = sb("QDb", [128, 2, 2, 8, 64])
        QD = [QDb[:, i] for i in range(2)]
        E0 = [sb(f"E0{i}", [128, 8, 128]) for i in range(2)]
        PT0 = sb("PT0", [128, 8, 128])
        nm0 = [sb(f"nm0{i}", [128, 8]) for i in range(2)]
        sum0 = [sb(f"sum0{i}", [128, 8]) for i in range(2)]
        rs0 = [sb(f"rs0{i}", [128, 8]) for i in range(2)]
        tmpo = [sb(f"tmpo{i}", [128, 2, 64]) for i in range(2)]
        AO = sb("AO", [128, 2, GB, 64])
        aos = [sb(f"aos{i}", [128, 2, GB, 64], F32R) for i in range(2)]
        yy = sb("yy", [128, 2, 256])
        ss = sb("ss", [128, 2])
        rr = sb("rr", [128, 2])
        ynT = [sb(f"ynT{i}", [128, 2, 256], F32R) for i in range(2)]
        hm = sb("hm", [128, 8, 256])
        gs = [sb(f"gs{i}", [128, 4, 256], F32R) for i in range(2)]
        X1 = [sb(f"X1{i}", [128, 256]) for i in range(4)]

        craw = sb("craw", [128, GB, 256])
        CH = [sb(f"CH{i}", [128, GB, 256], F32R) for i in range(2)]
        CL = [sb(f"CL{i}", [128, GB, 256], F32R) for i in range(2)]
        st6 = sb("st6", [128, 6])
        mv = sb("mv", [128, 2])
        mu = sb("mu", [128, 1])
        dd = sb("dd", [128, 1])
        ee = sb("ee", [128, 1])
        rstd = sb("rstd", [128, 1])
        aa = sb("aa", [128, 1])
        mb = sb("mb", [128, 1])
        bb = sb("bb", [128, 1])
        xnb = sb("xnb", [128, 2, 256])
        xnrm = [xnb[:, i] for i in range(2)]
        XS = [sb(f"XS{i}", [128, 256], F32R) for i in range(2)]
        QS = [sb(f"QS{i}", [128, 8, 256], F32R) for i in range(2)]
        VWb = sb("VWb", [128, 2, 2, 512])
        VW = [VWb[:, i] for i in range(2)]
        E1b = sb("E1b", [128, 4, 2, 256])
        E1 = [E1b[:, i] for i in range(4)]
        nm1 = [sb(f"nm1{i}", [128, 2]) for i in range(4)]
        sum1 = [sb(f"sum1{i}", [128, 2]) for i in range(4)]
        rs1 = [sb(f"rs1{i}", [128, 2]) for i in range(4)]
        PT1b = sb("PT1b", [128, 3, 2, 256])
        PT1 = [PT1b[:, i] for i in range(3)]

        sto = xnb[:, :, :]
        stk, stq = PT1b[:, 0:2], PT1b[:, 2]
        stw1 = hm[:, :, :].rearrange("p k n -> p (k n)").rearrange("p (k n) -> p k n", k=2)
        stage = VWb[:, :, :, :].rearrange("p a b c -> p (a b c)").rearrange("p (k n) -> p k n", k=8)
        l1w = E1b[0:64, :, :, :].rearrange("p w a n -> p w (a n)")
        y1 = [sb(f"y1{i}", [128, 256]) for i in range(2)]

        class Banks:

            def __init__(self, banks):
                self.idle = [(b, ()) for b in banks]

            def take(self):
                b, after = self.idle.pop(0)
                return b, after

            def give(self, b, *after):
                self.idle.append((b, after))

        BK = Banks(bank[0:7])
        OB = bank[7]

        def mm(out, lhsT, rhs, start, stop, *after, inc=False):
            return PE.do(lambda e: e.matmul(out, lhsT, rhs, start=start, stop=stop, skip_group_check=True), *after,
                         inc=inc)

        def three(out, a, b, start, stop, *after, inc=False):
            mm(out, a[0], b[0], start, False, *after)
            mm(out, a[0], b[1], False, False)
            return mm(out, a[1], b[0], False, stop, inc=inc)

        def f(ap):
            return ap.bitcast(F32)

        d_sm, d_q, d_kv, d_o, d_w1, d_w2, d_l1, d_mk = (sem(n) for n in
                                                        ("d_sm", "d_q", "d_kv", "d_o", "d_w1", "d_w2", "d_l1", "d_mk"))
        d_v = sem("d_v")
        d_h, d_x, d_c, d_out = sem("d_h"), sem("d_x"), sem("d_c"), [sem("d_out0"), sem("d_out1")]
        loads = {}

        def load_h(g, *after):
            loads["h", g] = SY.dma(lambda e: e.dma_start(
                hraw[:, :, :, :], hT[g].rearrange("p (k b t) -> p k b t", k=2, b=GB)), d_h, g + 1, *after)

        def load_mask(g, *after):
            loads["m", g] = SY.dma(lambda e: e.dma_start(mski[:, :, :], msk_d[:, g * GB:(g + 1) * GB, :]), d_mk, g + 1,
                                   *after)

        def load_x(g, *after):
            loads["x", g] = SY.dma(lambda e: e.dma_start(xnat[:, :, :], xn_d[g].rearrange("(u p) s -> p u s", p=128)),
                                   d_x, g + 1, *after)

        def load_ctx(g, *after):
            src = ctx_d[g * GB:(g + 1) * GB].rearrange("b c s -> c b s")
            SY.dma(lambda e: e.dma_start(craw[0:64, :, :], src), d_c, 2 * g + 1, *after)
            loads["c", g] = SY.dma(lambda e: e.dma_start(craw[64:128, :, :], src), d_c, 2 * g + 2)

        load_h(0)
        t_kw = SY.dma(lambda e: e.dma_start(stk[:, 0, :, :], kvw_d[0].rearrange("(k p) n -> p k n", p=128)), d_kv, 1)
        t_qw = SY.dma(lambda e: e.dma_start(stq[:, :, :], qw_d.rearrange("(k p) n -> p k n", p=128)), d_q, 1)
        t_vw = SY.dma(lambda e: e.dma_start(stk[:, 1, :, :], kvw_d[1].rearrange("(k p) n -> p k n", p=128)), d_v, 1)
        t_small = SY.dma(lambda e: e.dma_start(small[:, :], sm_d), d_sm, 1)
        load_mask(0)
        load_x(0)
        load_ctx(0)
        t_ow = SY.dma(lambda e: e.dma_start(sto[:, :, :], ow_d.rearrange("(k p) n -> p k n", p=128)), d_o, 1)
        t_w1 = SY.dma(lambda e: e.dma_start(stw1[:, :, :], w1_d.rearrange("(k p) n -> p k n", p=128)), d_w1, 1)
        t_w2 = SY.dma(lambda e: e.dma_start(stage[:, :, :], w2_d.rearrange("(k p) n -> p k n", p=128)), d_w2, 1)
        t_l1 = SY.dma(lambda e: e.dma_start(l1w[:, :, :], l1_d.rearrange("w o n -> o w n")), d_l1, 1)

        def split(hi, lo, src, *after):
            t = VE.do(lambda e: e.tensor_copy(hi, src), *after)
            return VE.do(lambda e: e.tensor_tensor(lo, src, f(hi), ALU.subtract), t)

        t_ones = PO.do(lambda e: e.memset(onesb[:, :], 1.0))
        PO.do(lambda e: e.memset(mrow[0][:, :, :], 0.0))
        t_mz = PO.do(lambda e: e.memset(mrow[1][:, :, :], 0.0))
        t_hh0 = split(hh[0][:, :, :, :], hh[1][:, :, :, :], hraw[:, :, :, :], loads["h", 0])
        t_wk = split(wk[0][:, :, :], wk[1][:, :, :], stk[:, 0, :, :], t_kw)
        t_wq = split(wq[0][:, :, :], wq[1][:, :, :], stq[:, :, :], t_qw)
        t_wv = split(wv[0][:, :, :], wv[1][:, :, :], stk[:, 1, :, :], t_vw)
        ready = {}

        def weights_late():
            ready["wo"] = split(wo[0][:, :, :], wo[1][:, :, :], sto[:, :, :], t_ow)
            b, fr = BK.take()
            vb = sm("vb")
            mm(b[:, 0:256], vb[:, 0:1].to_broadcast([128, 128]), sto[:, 0, :], True, False, t_ow, t_small, *fr)
            t = mm(b[:, 0:256], vb[:, 1:2].to_broadcast([128, 128]), sto[:, 1, :], False, True, inc=True)
            ready["obt"] = VE.do(lambda e: e.tensor_tensor(obt[:, :], b[:, 0:256], sm("ob"), ALU.add), t)
            BK.give(b, ready["obt"])
            yield
            pw = sm("pw")
            ts = [PO.do(lambda e, k=k: e.tensor_tensor(stw1[:, k, :], stw1[:, k, :], pw[:, k:k + 1].to_broadcast(
                [128, 1024]), ALU.mult), t_w1, t_small) for k in range(2)]
            yield
            for c in range(4):
                z = slice(256 * c, 256 * c + 256)
                ready["w1"] = split(w1[0][:, :, z], w1[1][:, :, z], stw1[:, :, z], *ts)
                yield
            for c in range(4):
                z = slice(2 * c, 2 * c + 2)
                ready["w2"] = split(w2[0][:, z, :], w2[1][:, z, :], stage[:, z, :], t_w2)
                yield

        def weights_l1():
            W = l1w[:, :, :].rearrange("o w (h c) -> o w h c", h=8)

            def both(b, col, n, lhsT, rhs, start, stop, *after, inc=False):
                for a in range(0, 128, 64):
                    t = mm(b[a:a + 64, col:col + n], lhsT, rhs, start, stop, *after, inc=inc and a == 64)
                return t
            bM, f1 = BK.take()
            for h in range(8):
                tM = both(bM, h * 64, 64, W[:, 0, h, :], W[:, 1, h, :], h == 0, h == 7,
                        t_l1, *f1, inc=h == 7)
            bV, f2 = BK.take()
            for h in range(8):
                tV = both(bV, h * 64, 64, W[:, 2, h, :], W[:, 3, h, :], h == 0, h == 7, *f2, inc=h == 7)
            bU, f3 = BK.take()
            bq, bv = sm("bq"), sm("bv")
            for h in range(8):
                both(bU, h, 1, W[:, 1, h, :], bq[0:64, h:h + 1], h == 0, h == 7, t_small, *f3)
            for h in range(8):
                tU = both(bU, 8, 1, W[:, 3, h, :], bv[0:64, h:h + 1], False, h == 7, inc=h == 7)
            t = VE.do(lambda e: e.tensor_scalar(MM[0][:, :], bM[:, :], 0.125, None, ALU.mult), tM)
            ready["M"] = VE.do(lambda e: e.scalar_tensor_tensor(MM[1][:, :], bM[:, :], 0.125, f(MM[0][:, :]),
                                                                ALU.mult, ALU.subtract), t)
            BK.give(bM, ready["M"])
            t1 = VE.do(lambda e: e.tensor_copy(WS[:, :], bV[:, :]), tV)
            ready["V"] = VE.do(lambda e: e.tensor_tensor(WS[64:128, :], bV[64:128, :], f(WS[64:128, :]),
                                                         ALU.subtract), t1)
            BK.give(bV, ready["V"])
            VE.do(lambda e: e.tensor_scalar(uu[:, :], bU[:, 0:8], 0.125, None, ALU.mult), tU)
            ready["u"] = VE.do(lambda e: e.tensor_tensor(cbias[:, :], bU[:, 8:9], sm("bo"), ALU.add))
            BK.give(bU, ready["u"])

        st = dict(hh=t_hh0, hh_free=(), kT_free=(), qT_free=(), vv_free=(), ao_free=(), aos_free=(), xo_free=(),
                  yn_free=(), ynT_free=(), hm_free=(), gl_free=())
        st["gs_free", 0] = st["gs_free", 1] = None
        qd_free, e0_free, pt0_free = [None, None], [None, None], [None, None]
        x1_ready, x1_free = {}, [(), (), (), ()]
        c_ready, c_free = {}, [(), ()]

        att = {}

        def pause(k):
            for _ in range(SP[k] if steady[0] else 1):
                yield

        steady, keep_free = [False], [0]

        def room(k):
            while len(BK.idle) < k + keep_free[0]:
                yield "wait"


        def layer0_att(g):
            keep = att[g] = {}
            t_mrow = VE.do(lambda e: e.tensor_scalar(mrow[g % 2][0:1, :, :], mski[:, :, :], 0.0, NEG, ALU.is_equal,
                                                     ALU.mult), loads["m", g], t_mz, qd_free[(GB - 1) % 2])
            if g == 0:
                thh = st["hh"]
            else:
                thh = split(hh[0][:, :, :, :], hh[1][:, :, :, :], hraw[:, :, :, :], loads["h", g], *st["hh_free"])
            if g + 1 < NG:
                load_h(g + 1, thh)
                load_mask(g + 1, t_mrow)
            yield from pause(0)
            tk = []
            for m in range(2):
                yield from room(1)
                b, fr = BK.take()
                for kt in range(2):
                    a = [w[:, kt, m * 128:(m + 1) * 128] for w in wk]
                    t = three(b[:, :], a, [x[:, kt, :, :] for x in hh], kt == 0, kt == 1, thh, t_wk, *fr, inc=kt == 1)
                yield from pause(1)
                kb = sm("kb")
                assert g == 0 or ("s1", GB - 1) in att[g - 1]
                tk.append(SC.do(lambda e, m=m, b=b: e.activation(kT[:, m, :, :], b[:, :].rearrange(
                    "p (b t) -> p b t", b=GB), ACT.Identity, bias=kb[:, m:m + 1], scale=1.0), t, t_small,
                    *st["kT_free"]))
                BK.give(b, tk[-1])
                yield from pause(2)
            yield from room(1)
            b, fr = BK.take()
            for m in range(2):
                for kt in range(2):
                    a = [w[:, kt, m * 128:(m + 1) * 128] for w in wq]
                    t = three(b[:, m * 256:(m + 1) * 256], a, [x[:, kt, :, 64:128] for x in hh],
                              m == 0 and kt == 0, kt == 1, t_wq, *fr, inc=kt == 1)
            yield from pause(3)
            for m in range(2):
                qb = sm("qb")
                assert g == 0 or ("qd", GB - 1, 1) in att[g - 1]
                tq = VE.do(lambda e, m=m, b=b: e.tensor_scalar(
                    qT[:, m, :, :], b[:, m * 256:(m + 1) * 256].rearrange("p (b t) -> p b t", b=GB),
                    qb[:, m:m + 1], 0.0625, ALU.add, ALU.mult), t, t_small, *st["qT_free"])
            BK.give(b, tq)
            yield from pause(4)
            tv = []
            for u in range(2):
                yield from room(1)
                b, fr = BK.take()
                for i in range(2):
                    for kt in range(2):
                        a = [x[:, kt, 2 * u + i, :] for x in hh]
                        t = three(b[:, i * 256:(i + 1) * 256], a, [w[:, kt, :] for w in wv],
                                  i == 0 and kt == 0, kt == 1, t_wv, *fr, inc=i == 1 and kt == 1)
                tlast = t
                yield from pause(5)
                assert g == 0 or ("o", GB - 1) in att[g - 1]
                tv.append(SC.do(lambda e, u=u, b=b: e.copy(
                    vv[:, 2 * u:2 * u + 2, :], b[:, :].rearrange("p (b n) -> p b n", b=2)), t, *st["vv_free"]))
                BK.give(b, tv[-1])
                yield from pause(6)
            st["hh_free"] = (tlast,)
            late = weights_late() if g == 0 else None
            yield from pause(7)

            def at_q(b, m):
                assert b < 2 or ("s1", b - 2) in keep
                r = b % 2
                E = PO if g or m == 0 else VE
                keep["qd", b, m] = E.do(lambda e: e.tensor_tensor(
                    QD[r][:, m, :, :], qT[:, m, b, :].unsqueeze(1).to_broadcast([128, 8, 64]),
                    sm("hm").unsqueeze(2).to_broadcast([128, 8, 64]), ALU.mult), tq, qd_free[r])
                if b == GB - 1 and m == 1:
                    st["qT_free"] = (keep["qd", b, 0], keep["qd", b, 1])

            def s_mm(b, m):
                r = b % 2
                pb, fr = BK.take()
                mm(pb[:, :].rearrange("p (j t) -> p j t", j=4)[:, :, 0:64], onesb[:, :],
                   mrow[g % 2][:, b, :].unsqueeze(1).to_broadcast([128, 4, 64]), True, False,
                   t_mrow, t_ones, keep["qd", b, m], tk[m], *fr)
                for j in range(4):
                    t = mm(pb[:, j * 128:(j + 1) * 128], QD[r][:, m, 2 * j:2 * j + 2, :], kT[:, m, b, :],
                           False, j == 3, inc=j == 3)
                if m == 1:
                    qd_free[r] = t
                    keep["s1", b] = t
                    if b == GB - 1:
                        st["kT_free"] = (t,)
                keep["s", b] = (pb, t)

            def s_max(b, m):
                assert b < 2 or ("t1", b - 2) in keep
                r = b % 2
                pb, t = keep["s", b]
                keep["m", b] = VE.do(lambda e: e.tensor_reduce(
                    nm0[r][:, 4 * m:4 * m + 4], pb[:, :].rearrange("p (j t) -> p j t", j=4), AX.X, ALU.max,
                    negate=True), t, e0_free[r])

            def s_exp(b, m):
                r = b % 2
                pb, t = keep["s", b]
                for j in range(4):
                    jj = 4 * m + j
                    t2 = SC.do(lambda e, j=j, jj=jj: e.activation(
                        E0[r][:, jj, :], pb[:, j * 128:(j + 1) * 128], ACT.Exp, bias=nm0[r][:, jj:jj + 1],
                        scale=1.0, accum_out=sum0[r][:, jj:jj + 1]), keep["m", b], e0_free[r])
                BK.give(pb, t2)
                keep["e", b] = t2

            def at_n(b, m):
                r, c = b % 2, slice(4 * m, 4 * m + 4)
                t = VE.do(lambda e: e.reciprocal(rs0[r][:, c], sum0[r][:, c]), keep["e", b])
                E = PO if g or m == 0 else VE
                keep["n", b, m] = E.do(lambda e: e.tensor_tensor(
                    E0[r][:, c, :], E0[r][:, c, :], rs0[r][:, c].unsqueeze(2).to_broadcast([128, 4, 128]),
                    ALU.mult), t)

            def t_mm(b, m):
                r = b % 2
                pb, fr = BK.take()
                for j in range(4):
                    t = PE.do(lambda e, j=j: e.transpose(pb[:, j * 128:(j + 1) * 128], E0[r][:, 4 * m + j, :],
                                                         sm("ident")), keep["n", b, m], *fr, inc=j == 3)
                if m == 1:
                    e0_free[r] = t
                    keep["t1", b] = t
                keep["tp", b] = (pb, t)

            def t_ev(b, m):
                assert b < 1 or ("o", b - 1) in keep
                pb, t = keep["tp", b]
                tt = SC.do(lambda e: e.copy(PT0[:, 4 * m:4 * m + 4, :], pb[:, :].rearrange(
                    "p (j t) -> p j t", j=4)), t, pt0_free[0])
                BK.give(pb, tt)
                keep["t", b] = tt

            def v_mm(b):
                pb, fr = BK.take()
                for m in range(2):
                    for j in range(4):
                        t = mm(pb[32 * j:32 * j + 32, m * 128:(m + 1) * 128],
                               vv[:, b, 128 * m + 32 * j:128 * m + 32 * j + 32], PT0[:, 4 * m + j, :],
                               m == 0, m == 1, tv[b // 2], keep["t", b], *fr, inc=m == 1 and j == 3)
                pt0_free[0] = t
                if b == GB - 1:
                    st["vv_free"] = (t,)
                keep["o", b] = (pb, t)

            def v_ev(b, which):
                r = b % 2
                pb, t = keep["o", b]
                o = pb[:, 0:256].rearrange("p (m h q) -> p m h q", m=2, h=2)
                par = sm("par")
                if which == 0:
                    assert b < 2 or ("ao", b - 2) in keep
                    keep["o2", b] = SC.do(lambda e: e.activation(tmpo[r][:, :, :], o[:, :, 0, :], ACT.Copy, bias=0.0,
                                                                 scale=par[:, 0:1]), t, keep.get(("ao", b - 2)))
                    return
                assert g == 0 or "aos" in att[g - 1]
                t3 = VE.do(lambda e: e.scalar_tensor_tensor(AO[:, :, b, :], o[:, :, 1, :], par[:, 1:2],
                                                            tmpo[r][:, :, :], ALU.mult, ALU.add), keep["o2", b],
                           *st["ao_free"])
                BK.give(pb, t3)
                keep["ao", b] = t3

            acts = [lambda b: at_q(b, 0), lambda b: at_q(b, 1), lambda b: s_mm(b, 0), lambda b: s_max(b, 0),
                    lambda b: s_exp(b, 0), lambda b: at_n(b, 0), lambda b: s_mm(b, 1), lambda b: s_max(b, 1),
                    lambda b: s_exp(b, 1), lambda b: at_n(b, 1), lambda b: t_mm(b, 0), lambda b: t_ev(b, 0),
                    lambda b: t_mm(b, 1), lambda b: t_ev(b, 1), lambda b: v_mm(b), lambda b: v_ev(b, 0),
                    lambda b: v_ev(b, 1)]
            mic = MIC if g else MIC0
            off = OFF if g else OFF0
            need = {2: 1, 6: 1, 10: 1, 12: 1, 14: 1}
            for i in range(off * (GB - 1) + mic[-1] + 1):
                yield from room(sum(need.get(k, 0) for k, at in enumerate(mic) for b in range(GB) if at == i - off * b))
                for b in range(GB):
                    for at, act in zip(mic, acts):
                        if at == i - off * b:
                            act(b)
                if late and i % LATE == LATE - 1:
                    next(late, None)
                yield from pause(8)
            for _ in late or ():
                pass

        def layer0_mlp(g):
            keep = att[g]
            t_xo = PO.do(lambda e: e.tensor_tensor(xo[:, :, :], xnat[:, :, :], obt[:, :].unsqueeze(1).to_broadcast(
                [128, 2, 256]), ALU.add), loads["x", g], ready["obt"], *st["xo_free"])
            t_xb = PO.do(lambda e: e.tensor_tensor(xnat[:, :, :], xnat[:, :, :], sm("b2").unsqueeze(1).to_broadcast(
                [128, 2, 256]), ALU.add), t_xo)
            t = split(aos[0][:, :, :, :], aos[1][:, :, :, :], AO[:, :, :, :], keep["ao", GB - 1], *st["aos_free"])
            st["ao_free"] = (t,)
            keep["aos"] = t
            yield from pause(9)
            yield from room(1)
            pb, fr = BK.take()
            for u in range(2):
                for kt in range(2):
                    a = [x[:, kt, 2 * u:2 * u + 2, :] for x in aos]
                    t1 = three(pb[:, u * 256:(u + 1) * 256], a, [w[:, kt, :] for w in wo], u == 0 and kt == 0,
                               kt == 1, t, ready["wo"], *fr, inc=u == 1 and kt == 1)
            st["aos_free"] = (t1,)
            yield from pause(10)
            t = VE.do(lambda e, pb=pb: e.tensor_tensor(yy[:, :, :], pb[:, :].rearrange("p (u n) -> p u n", u=2), xo[:, :, :],
                                                ALU.add), t1, t_xo)
            BK.give(pb, t)
            for u in range(2):
                tt = VE.do(lambda e, u=u: e.tensor_tensor_reduce(
                    xo[:, u, :], yy[:, u, :], yy[:, u, :], 1.0 / 256, 0.0, ALU.mult, ALU.add, ss[:, u:u + 1]), t)
                t = tt
            st["xo_free"] = (t,)
            t = VE.do(lambda e: e.tensor_scalar(rr[:, :], ss[:, :], 1e-6, None, ALU.add), t)
            t = PO.do(lambda e: e.tensor_tensor(rr[:, :], rr[:, :], sm("mh"), ALU.pow), t)
            yield from pause(11)
            for u in range(2):
                tn = VE.do(lambda e, u=u: e.tensor_scalar(yy[:, u, :], yy[:, u, :], rr[:, u:u + 1], None, ALU.mult),
                           t, *st["yn_free"])
            yield from pause(12)
            yield from room(1)
            pb, fr = BK.take()
            for kt in range(2):
                for u in range(2):
                    t = PE.do(lambda e, kt=kt, u=u, pb=pb: e.transpose(pb[:, kt * 256 + u * 128:kt * 256 + u * 128 + 128],
                                                                yy[:, u, kt * 128:(kt + 1) * 128], sm("ident")),
                              tn, *fr, inc=kt == 1 and u == 1)
            st["yn_free"] = (t,)
            yield from pause(13)
            src = pb[:, :].rearrange("p (k t) -> p k t", k=2)
            t1 = SC.do(lambda e: e.copy(ynT[0][:, :, :], src), t, *st["ynT_free"])
            tT = VE.do(lambda e: e.tensor_tensor(ynT[1][:, :, :], src, f(ynT[0][:, :, :]), ALU.subtract), t1)
            BK.give(pb, tT)
            yield from pause(14)
            b1 = sm("b1")
            for c in range(4):
                yield from room(1)
                pb, fr = BK.take()
                for i in range(2):
                    m = 2 * c + i
                    for kt in range(2):
                        a = [w[:, kt, m * 128:(m + 1) * 128] for w in w1]
                        t = three(pb[:, i * 256:(i + 1) * 256], a, [x[:, kt, :] for x in ynT], i == 0 and kt == 0,
                                  kt == 1, tT, ready["w1"], *fr, inc=i == 1 and kt == 1)
                st["ynT_free"] = (t,)
                yield from pause(15)
                tb = VE.do(lambda e, c=c, pb=pb: e.tensor_tensor(
                    hm[:, 2 * c:2 * c + 2, :], pb[:, :].rearrange("p (i t) -> p i t", i=2),
                    b1[:, 2 * c:2 * c + 2].unsqueeze(2).to_broadcast([128, 2, 256]), ALU.add), t, *st["hm_free"])
                BK.give(pb, tb)
                yield from pause(16)
            tg = SC.do(lambda e: e.activation(hm[:, :, :], hm[:, :, :], ACT.Gelu_apprx_tanh), tb, *st["gl_free"])
            yield from pause(17)
            yield from room(1)
            pb, fr = BK.take()
            gs_ready = {}
            for c in range(6):
                if c >= 2:
                    d = c - 2
                    for u in range(2):
                        for kt in range(2 * d, 2 * d + 2):
                            a = [x[:, kt % 4, u * 128:(u + 1) * 128] for x in gs]
                            t = three(pb[:, u * 256:(u + 1) * 256], a, [w[:, kt, :] for w in w2], kt == 0 and u == 0,
                                      kt == 7, gs_ready[d], ready["w2"], *fr, inc=kt % 2 == 1)
                    st["gs_free", d % 2] = t
                    yield from pause(18)
                if c < 4:
                    z = slice(2 * (c % 2), 2 * (c % 2) + 2)
                    t = VE.do(lambda e, c=c, z=z: e.tensor_copy(gs[0][:, z, :], hm[:, 2 * c:2 * c + 2, :]), tg,
                              st["gs_free", c % 2])
                    gs_ready[c] = (PO if g or c % 2 == 0 else VE).do(lambda e, c=c, z=z: e.tensor_tensor(
                        gs[1][:, z, :], hm[:, 2 * c:2 * c + 2, :], f(gs[0][:, z, :]), ALU.subtract), t)
                    yield from pause(19)
            yield from pause(20)
            st["hm_free"] = (gs_ready[2], gs_ready[3])
            for u in range(2):
                p = 2 * g + u
                x1_ready[p] = VE.do(lambda e, u=u, p=p: e.tensor_tensor(
                    X1[p % 4][:, :], pb[:, u * 256:(u + 1) * 256], xnat[:, u, :], ALU.add), t, t_xb, *x1_free[p % 4])
            BK.give(pb, x1_ready[2 * g + 1])
            cs = g % 2
            t1 = VE.do(lambda e: e.tensor_copy(CH[cs][:, :, :], craw[:, :, :]), loads["c", g], *c_free[cs])
            c_ready[g] = PO.do(lambda e: e.tensor_tensor(CL[cs][:, :, :], craw[:, :, :], f(CH[cs][:, :, :]),
                                                         ALU.subtract), t1, *c_free[cs])
            yield from pause(21)
            if g + 1 < NG:
                load_x(g + 1, x1_ready[2 * g + 1])
                load_ctx(g + 1, c_ready[g])
            yield from pause(22)

        xn_ready, qs_ready, vw_ready = {}, {}, {}
        xnrm_free, xs_free, qs_free, vw_free = [(), ()], [(), ()], [(), ()], [(), ()]

        def norm_pair(p):
            x = X1[p % 4]
            t = VE.do(lambda e: e.bn_stats(st6[:, :], x[:, :]), x1_ready[p])
            tm = VE.do(lambda e: e.bn_aggr(mv[:, :], st6[:, :]), t)
            yield from pause(23)
            yield from room(1)
            pb, fr = BK.take()
            t = mm(pb[:, 0:1], sm("avg"), mv[:, 0:1], True, True, tm, t_small, *fr, inc=True)
            yield from pause(24)
            tmu = VE.do(lambda e: e.tensor_copy(mu[:, :], pb[:, 0:1]), t)
            t = VE.do(lambda e: e.tensor_tensor(dd[:, :], mv[:, 0:1], mu[:, :], ALU.subtract), tmu)
            t = VE.do(lambda e: e.scalar_tensor_tensor(ee[:, :], dd[:, :], dd[:, 0:1], mv[:, 1:2], ALU.mult, ALU.add),
                      t)
            yield from pause(25)
            t = mm(pb[:, 2:3], sm("avg"), ee[:, :], True, True, t, inc=True)
            yield from pause(26)
            t = VE.do(lambda e: e.tensor_scalar(rstd[:, :], pb[:, 2:3], 1e-5, None, ALU.add), t)
            BK.give(pb, t)
            t = PO.do(lambda e: e.tensor_tensor(rstd[:, :], rstd[:, :], sm("mh")[:, 0:1], ALU.pow), t)
            yield from pause(27)
            t = VE.do(lambda e: e.tensor_tensor(aa[:, :], rstd[:, :], sm("gamma"), ALU.mult), t)
            t = VE.do(lambda e: e.tensor_tensor(mb[:, :], mu[:, :], aa[:, :], ALU.mult), t)
            t = VE.do(lambda e: e.tensor_tensor(bb[:, :], sm("beta"), mb[:, :], ALU.subtract), t)
            xn_ready[p] = VE.do(lambda e: e.tensor_scalar(xnrm[p % 2][:, :], x[:, :], aa[:, 0:1], bb[:, 0:1],
                                                          ALU.mult, ALU.add), t, *xnrm_free[p % 2])
            yield from pause(28)

        def prep(n):
            p, o, s, g, bg = n // 2, 64 * (n % 2), n % 2, n // GB, n % GB
            if p not in xn_ready:
                yield from norm_pair(p)
            q = 64 - o
            xr = xnrm[p % 2]
            yield from pause(29)
            t = SC.do(lambda e: e.copy(XS[s][o:o + 64, :], xr[o:o + 64, :]), xn_ready[p], *xs_free[s])
            yield from pause(30)
            txs = VE.do(lambda e: e.tensor_tensor(XS[s][q:q + 64, :], xr[o:o + 64, :], f(XS[s][o:o + 64, :]),
                                                  ALU.subtract), t)
            if n % 2 == 1:
                xnrm_free[p % 2] = (txs,)
            yield from pause(31)
            ch, cl = CH[g % 2], CL[g % 2]
            for c in range(2):
                yield from room(1)
                pb, fr = BK.take()
                for i in range(2):
                    pr = 2 * c + i
                    sl = pb[:, i * 256:(i + 1) * 256]
                    mm(sl, MM[0][:, pr * 128:(pr + 1) * 128], XS[s][:, :], i == 0, False, txs, ready["M"],
                       ready["u"], *fr)
                    t = mm(sl, MM[1][:, pr * 128:(pr + 1) * 128], XS[s][:, :], False, True, inc=i == 1)
                tlast = t
                yield from pause(32)
                where = [(4 * c + j, 64 * (j % 2), pb[64 * (j % 2):64 * (j % 2) + 64, 256 * (j // 2):256 * (j // 2) + 256])
                         for j in range(4)]
                for d in range(2):
                    for h, a, sl in where[2 * d:2 * d + 2]:
                        th = SC.do(lambda e, h=h, a=a, sl=sl: e.activation(
                            QS[s][a:a + 64, h, :], sl, ACT.Identity, bias=uu[a:a + 64, h:h + 1], scale=1.0),
                            t, *qs_free[s])
                    yield from pause(33)
                for d in range(2):
                    for h, a, sl in where[2 * d:2 * d + 2]:
                        z = 64 - a
                        tl = VE.do(lambda e, h=h, a=a, z=z, sl=sl: e.scalar_tensor_tensor(
                            QS[s][z:z + 64, h, :], sl, uu[a:a + 64, h:h + 1], f(QS[s][a:a + 64, h, :]), ALU.add,
                            ALU.subtract), th, *qs_free[s])
                        qs_ready[n, h] = tl
                    yield from pause(34)
                BK.give(pb, tl)
                yield from pause(35)
            xs_free[s] = (tlast,)
            while n >= 2 and ("v", n - 2) not in hs:
                yield "wait"
            tv = []
            for j in range(2):
                yield from room(1)
                pb, fr = BK.take()
                mm(pb[:, :], ch[:, bg, j * 128:(j + 1) * 128], WS[:, :], True, False, ready["V"], c_ready[g], *fr)
                t = mm(pb[:, :], cl[:, bg, j * 128:(j + 1) * 128], WS[:, :], False, True, inc=True)
                yield from pause(36)
                E = (SC, VE)[j]
                tv.append(E.do((lambda e, pb=pb: e.copy(VW[s][:, 0, :], pb[:, :])) if j == 0 else
                               (lambda e, pb=pb: e.tensor_copy(VW[s][:, 1, :], pb[:, :])), t, *vw_free[s]))
                BK.give(pb, tv[-1])
            vw_ready[n] = tv
            yield from pause(37)

        e1_free, pt1_free, hs = [None] * 4, [None] * 3, {}
        o_free, yo_free = [None, None], [None, None]

        def stage_s(t_):
            n, h = divmod(t_, 8)
            s, g, bg, r = n % 2, n // GB, n % GB, t_ % 4
            pb, fr = BK.take()
            for i in range(2):
                a = QS[s][:, h, i * 128:(i + 1) * 128]
                mm(pb[:, i * 256:(i + 1) * 256], a, CH[g % 2][:, bg, :], i == 0, False, qs_ready[n, h], *fr)
                t = mm(pb[:, i * 256:(i + 1) * 256], a, CL[g % 2][:, bg, :], False, True, inc=i == 1)
            if h == 7:
                qs_free[s] = (t,)
                if bg == GB - 1:
                    hs["c", g] = t
            hs["s", t_] = (pb, t)

        def stage_x(t_):
            assert t_ < 4 or ("e", t_ - 4) in hs
            r = t_ % 4
            pb, t = hs["s", t_]
            hs["m", t_] = VE.do(lambda e: e.tensor_reduce(nm1[r][:, :], pb[:, :].rearrange("p (i t) -> p i t", i=2), AX.X,
                                                ALU.max, negate=True), t, e1_free[r])

        def stage_e(t_):
            assert t_ < 4 or (("tp", t_ - 4) in hs and ("n", t_ - 4) in hs)
            r = t_ % 4
            pb, t = hs["s", t_]
            for i in range(2):
                t2 = SC.do(lambda e, i=i: e.activation(E1[r][:, i, :], pb[:, i * 256:(i + 1) * 256], ACT.Exp,
                                                       bias=nm1[r][:, i:i + 1], scale=1.0,
                                                       accum_out=sum1[r][:, i:i + 1]), hs["m", t_], e1_free[r])
            BK.give(pb, t2)
            hs["e", t_] = t2

        def stage_n(t_):
            r = t_ % 4
            t = VE.do(lambda e: e.reciprocal(rs1[r][:, :], sum1[r][:, :]), hs["e", t_])
            hs["n", t_] = PO.do(lambda e: e.tensor_tensor(
                E1[r][:, :, :], E1[r][:, :, :], rs1[r][:, :].unsqueeze(2).to_broadcast([128, 2, 256]), ALU.mult), t)

        def stage_t(t_):
            r = t_ % 4
            pb, fr = BK.take()
            for j in range(2):
                for i in range(2):
                    t = PE.do(lambda e, i=i, j=j: e.transpose(
                        pb[:, j * 256 + i * 128:j * 256 + i * 128 + 128], E1[r][:, i, j * 128:(j + 1) * 128],
                        sm("ident")), hs["n", t_], *fr, inc=i == 1 and j == 1)
            e1_free[r] = t
            hs["tp", t_] = (pb, t)

        def stage_u(t_):
            assert t_ < 3 or ("pv", t_ - 3) in hs
            r3 = t_ % 3
            pb, t = hs["tp", t_]
            src = pb[:, :].rearrange("p (j t) -> p j t", j=2)
            if EV[t_ % 8] or t_ >= UA[0] and t_ % 4 == 1 or t_ >= UA[1] and t_ % 4 == 2:
                t2 = SC.do(lambda e: e.copy(PT1[r3][:, :, :], src), t, pt1_free[r3])
            else:
                t2 = VE.do(lambda e: e.tensor_copy(PT1[r3][:, :, :], src), t, pt1_free[r3])
            BK.give(pb, t2)
            hs["t", t_] = t2

        def stage_v(t_):
            if t_ % 2 == 0:
                return
            n, s = t_ // 8, (t_ // 8) % 2
            for j in range(2):
                for tt in (t_ - 1, t_):
                    h, c = tt % 8, 64 * (tt % 2)
                    t = mm(OB[c:c + 64, s * 256:(s + 1) * 256], VW[s][:, j, h * 64:(h + 1) * 64],
                           PT1[tt % 3][:, j, :], h < 2 and j == 0, h >= 6 and j == 1,
                           hs["t", tt], vw_ready[n][j], o_free[0], inc=j == 1)
                    pt1_free[tt % 3] = hs["pv", tt] = t
            if t_ % 8 == 7:
                vw_free[s] = (t,)
                hs["v", n] = t

        def finish(n):
            p, a, s = n // 2, 64 * (n % 2), n % 2
            x = X1[p % 4]
            o = OB[:, s * 256:(s + 1) * 256]
            t = VE.do(lambda e: e.scalar_tensor_tensor(y1[p % 2][a:a + 64, :], o[a:a + 64, :], cbias[a:a + 64, 0:1],
                                                       x[a:a + 64, :], ALU.add, ALU.add), hs["v", n], yo_free[p % 2],
                      ready["u"])
            z = 64 - a
            t = VE.do(lambda e: e.tensor_tensor(y1[p % 2][a:a + 64, :], o[z:z + 64, :], y1[p % 2][a:a + 64, :],
                                                ALU.add), t, None)
            o_free[0] = t
            if s == 1:
                x1_free[p % 4] = (t,)
                yo_free[p % 2] = SY.dma(lambda e: e.dma_start(out_d[2 * p:2 * p + 2].rearrange("b c s -> (b c) s"),
                                                              y1[p % 2][:, :]), d_out[p % 2], p // 2 + 1, t)

        CH0, CH1, LE, LN, LT, LU, LV = CFG
        a, na, nb = layer0_att(1), 0, 0
        for k, _ in enumerate(layer0_att(0)):
            if k >= HEAD[0] and na < 2 or k >= HEAD[3] and na < HEAD[5]:
                na += 1
                next(a, None)
        b, na = layer0_mlp(0), 0
        for _ in b:
            if nb == L1AT:
                weights_l1()
            nb += 1
            while na < HEAD[2] * nb / HEAD[1]:
                na += 1
                next(a, None)
        for _ in prep(0):
            if na < HEAD[2] + HEAD[6]:
                na += 1
                next(a, None)
        T = NB * 8
        stages = [(0, stage_s), (LX, stage_x), (LE, stage_e), (LN, stage_n), (LT, stage_t), (LU, stage_u), (LV, stage_v)]
        stages = [stages[i] for i in ORD]
        steady[0], keep_free[0] = True, RES
        turn = {j: 8 * GB * (j - 1) + SH[j - 1] for j in range(1, NG)}
        work = {"att": [a, 0, CHA * HEAD[4] / 100, 0, 7 * turn[1]]}

        pos = [0]
        for at in range(7 * T + 1):
            t_ = at // 7
            j = t_ // (8 * GB) + 1
            pos.append(pos[-1] + (1 if j < NG and turn[j] <= t_ < 8 * GB * (j - 1) + CUT else WA))

        def run(key, at):
            w = work.get(key)
            if w is not None:
                a, b = w[3], w[4]
                part = (pos[at + 1] - pos[a]) / (pos[b] - pos[a]) if key == "att" else (at - a + 1) / (b - a)
                while w[1] < w[2] * part:
                    if next(w[0], None) == "wait":
                        break
                    w[1] += 1

        def complete(key):
            w = work.pop(key, None)
            if w is None:
                return
            keep_free[0] = 0
            for k, v in enumerate(w[0]):
                assert k < 500
                if v == "wait":
                    for o in work.values():
                        o[1] += next(o[0], None) != "wait"
            keep_free[0] = RES

        for t_ in range(T + LV):
            n, h = divmod(t_, 8)
            g, tg = divmod(t_, 8 * GB)
            for j in range(1, NG):
                if t_ == turn[j]:
                    complete("att")
                    if g >= 1:
                        c_free[j % 2] = (hs["c", g - 1],)
                    work["mlp"] = [layer0_mlp(j), 0, CH0, 7 * t_, 7 * (8 * GB * (j - 1) + CUT)]
                    if j + 1 < NG:
                        work["att"] = [layer0_att(j + 1), 0, CHA, 7 * (t_ + BEG), 7 * turn[j + 1]]
            for i, (lag, step) in enumerate(stages):
                if 0 <= t_ - lag < T:
                    step(t_ - lag)
                    if step is stage_v and (t_ - lag) % 8 == 7:
                        finish((t_ - lag) // 8)
                for key in [("mlp", "att", "prep")[k] for k in PRI] if t_ < T else ():
                    run(key, 7 * t_ + i)
                if n + 1 < NB and "prep" not in work and i == 6 and h < 7 and (n % GB < GB - 1 or "mlp" not in work):
                    work["prep"] = [prep(n + 1), 0, CH1, 7 * t_ + i + 1, 7 * (8 * n + 8)]
            if tg == CUT - 1:
                complete("mlp")
            if h == 7:
                complete("prep")

        SY.do(None, (d_out[0], 16 * (NB // 4)), (d_out[1], 16 * (NB // 4)), inc=False)

        block = es.enter_context(nc.Block())

        @block.sync
        def _(e):
            SY.play(e)

        @block.tensor
        def _(e):
            PE.play(e)

        @block.vector
        def _(e):
            VE.play(e)

        @block.scalar
        def _(e):
            SC.play(e)

        @block.gpsimd
        def _(e):
            PO.play(e)


def kernel(x, ctx_2048, mask_BxS2_ik0, L0_xattn_q_w, L0_xattn_q_b, L0_xattn_kv_w, L0_xattn_kv_b, L0_xattn_out_w,
           L0_xattn_out_b, L0_xattn_postnorm_w, L0_xattn_mlp_w1, L0_xattn_mlp_b1, L0_xattn_mlp_w2, L0_xattn_mlp_b2,
           L1_xattn_gamma, L1_xattn_beta, L1_xattn_Wq, L1_xattn_bq, L1_xattn_Wkv, L1_xattn_bkv, L1_xattn_Wo,
           L1_xattn_bo):
    import numpy as np
    import concourse.bacc as bacc
    from concourse.bass_utils import run_bass_kernel_spmd

    asc = np.ascontiguousarray
    x = np.asarray(x)
    ctx = np.asarray(ctx_2048)
    h = np.concatenate([ctx, x], axis=1).reshape(NG, GB, 128, 2, 128)
    hT = asc(h.transpose(0, 4, 3, 1, 2)).reshape(NG, 128, 2 * GB * 128)
    kvw = asc(np.asarray(L0_xattn_kv_w).reshape(256, 256, 2).transpose(2, 0, 1))
    kvb = np.asarray(L0_xattn_kv_b).reshape(256, 2)
    wkv = np.asarray(L1_xattn_Wkv).reshape(2, 8, 64, 64)

    def heads(w):
        return np.asarray(w).reshape(8, 64, 64).transpose(1, 0, 2).reshape(64, 512)
    l1 = asc(np.stack([heads(L1_xattn_Wq), heads(wkv[0]), heads(wkv[1]), heads(np.asarray(L1_xattn_Wo).T)]))

    small = np.zeros((128, SMW), np.float32)

    def put(name, a):
        o, n = SM[name]
        small[:, o:o + n] = a
    put("qb", np.asarray(L0_xattn_q_b).reshape(2, 128).T)
    put("kb", kvb[:, 0].reshape(2, 128).T)
    put("vb", kvb[:, 1].reshape(2, 128).T)
    put("b1", np.asarray(L0_xattn_mlp_b1).reshape(8, 128).T)
    put("pw", np.asarray(L0_xattn_postnorm_w).reshape(2, 128).T)

    def twice(a):
        a = np.asarray(a)
        return np.concatenate([a, a], axis=0)
    put("gamma", twice(L1_xattn_gamma)[:, None])
    put("beta", twice(L1_xattn_beta)[:, None])
    put("bo", twice(L1_xattn_bo)[:, None])
    put("bq", twice(np.asarray(L1_xattn_bq).reshape(8, 64).T))
    bkv = np.asarray(L1_xattn_bkv).reshape(2, 8, 64)
    put("bv", twice(bkv[1].T))
    p = np.arange(128)
    put("par", ((p[:, None] // 16) % 2 == np.arange(2)[None, :]).astype(np.float32))
    put("hm", (p[:, None] // 16 == np.arange(8)[None, :]).astype(np.float32))
    put("ob", np.asarray(L0_xattn_out_b)[None, :])
    put("b2", np.asarray(L0_xattn_mlp_b2)[None, :])
    put("mh", np.float32(-0.5))
    put("ident", np.eye(128, dtype=np.float32))
    put("avg", np.where(p[:, None] // 64 == p[None, :] // 64, np.float32(1 / 64), np.float32(0)))

    arrays = {
        "hT": hT, "xn": asc(x.reshape(NG, 256, 256)), "ctx": asc(ctx),
        "msk": asc(np.asarray(mask_BxS2_ik0)).reshape(1, NB, 64), "qw": asc(L0_xattn_q_w), "kvw": kvw,
        "ow": asc(L0_xattn_out_w), "w1": asc(L0_xattn_mlp_w1), "w2": asc(L0_xattn_mlp_w2), "l1": l1, "sm": small,
    }
    nc = bacc.Bacc("TRN2", target_bir_lowering=False, num_devices=1)
    args = [nc.dram_tensor(f"in_{k}", a.shape, mybir.dt.from_np(a.dtype), kind="ExternalInput").ap()
            for k, a in arrays.items()]
    out = nc.dram_tensor("out_0", (NB, 64, 256), F32, kind="ExternalOutput").ap()
    build(nc, *args, out)
    r = run_bass_kernel_spmd(nc, [{f"in_{k}": a for k, a in arrays.items()}], core_ids=[0])
    return r.results[0]["out_0"]
```
